# Optimizing a Trainium2 kernel written in Bass

```python
import numpy as np
import jax
import jax.numpy as jnp

def _softmax(x, axis=-1):
    return jax.nn.softmax(x, axis=axis)

def _gelu(x):
    return jax.nn.gelu(x, approximate=True)

def _silu(x):
    return jax.nn.silu(x)

def _sigmoid(x):
    return jax.nn.sigmoid(x)

def _layernorm(x, axis=-1, eps=1e-05):
    m = jnp.mean(x, axis=axis, keepdims=True)
    v = jnp.var(x, axis=axis, keepdims=True)
    return (x - m) / jnp.sqrt(v + eps)

def _scatter_add(tgt, idx, src, axis=0):
    return tgt.at[idx].add(src)

def _segment_sum(src, seg, n):
    return jax.ops.segment_sum(src, seg, n)
kernel_name = 'mk_adj_preln_d4_adj_r2_740d5d'

def setup_inputs(seed: int=0):
    np.random.seed(seed)
    _w = jnp.asarray

    def _rec_inputs():
        import jax
        import jax.numpy as jnp
        _gk = jax.random.key(seed)
        x = -0.0005207 + 1.001 * jax.random.normal(jax.random.fold_in(_gk, 1), (1354, 256), jnp.float32)
        _a = jax.random.bernoulli(jax.random.fold_in(_gk, 2), 0.00295421, (1354, 1354))
        _a = jnp.logical_or(_a, jnp.swapaxes(_a, -1, -2))
        _a = jnp.logical_or(_a, jnp.eye(1354, dtype=bool))
        _af = _a.astype(jnp.float32)
        adj = _af
        return (x, adj)
    x, adj = _rec_inputs()

    def _L0_gnn_setup():
        import jax, jax.numpy as jnp
        import numpy as np
        N = 2048
        D = 256
        H = 4
        NEG = -10000000000.0
        ALPHA = 0.3
        key = jax.random.key(seed)
        ks = jax.random.split(key, 8)
        nodes = jax.random.normal(ks[0], (N, D), dtype=jnp.float32)
        adj = (jax.random.uniform(ks[1], (N, N)) < 0.01).astype(jnp.float32)
        adj = jnp.maximum(adj, jnp.eye(N, dtype=jnp.float32))
        s = 0.05
        W_node = jax.random.normal(ks[2], (D, D), dtype=jnp.float32) * s
        b_node = jnp.zeros((D,), dtype=jnp.float32)
        K = jax.random.normal(ks[3], (H, D, D), dtype=jnp.float32) * s
        A_self = jax.random.normal(ks[4], (H, D), dtype=jnp.float32) * s
        A_neigh = jax.random.normal(ks[5], (H, D), dtype=jnp.float32) * s
        return {'nodes': nodes, 'adj': adj, 'W_node': W_node, 'b_node': b_node, 'K': K, 'A_self': A_self, 'A_neigh': A_neigh, 'num_heads': H}
    _L0_gnn_all = _L0_gnn_setup()
    _L0_gnn_in = {k: v for k, v in _L0_gnn_all.items() if k in ('W_node', 'b_node', 'K', 'A_self', 'A_neigh')}
    del _L0_gnn_all

    def _L1_gnn_setup():
        import jax, jax.numpy as jnp
        import numpy as np
        N = 4096
        D = 256
        key = jax.random.key(seed)
        ks = jax.random.split(key, 6)
        s = 1.0 / np.sqrt(D)
        return {'x': jax.random.normal(ks[0], (N, D), jnp.float32), 'spatial_encoding': jax.random.normal(ks[1], (N, N), jnp.float32), 'edge_encoding': jax.random.normal(ks[2], (N, N), jnp.float32), 'Wq': jax.random.normal(ks[3], (D, D), jnp.float32) * s, 'bq': jnp.zeros((D,), jnp.float32), 'Wk': jax.random.normal(ks[4], (D, D), jnp.float32) * s, 'bk': jnp.zeros((D,), jnp.float32), 'Wv': jax.random.normal(ks[5], (D, D), jnp.float32) * s, 'bv': jnp.zeros((D,), jnp.float32)}
    _L1_gnn_all = _L1_gnn_setup()
    _L1_gnn_in = {k: v for k, v in _L1_gnn_all.items() if k in ('Wq', 'bq', 'Wk', 'bk', 'Wv', 'bv')}
    del _L1_gnn_all

    def _L2_gnn_setup():
        import jax, jax.numpy as jnp
        import numpy as np
        N = 5000
        IN_F = 256
        OUT_F = 256
        key = jax.random.key(seed)
        k1, k2, k3 = jax.random.split(key, 3)
        x = jax.random.normal(k1, (N, IN_F), dtype=jnp.float32)
        adj = jax.random.uniform(k2, (N, N), dtype=jnp.float32)
        stdv = 1.0 / np.sqrt(OUT_F)
        weight = jax.random.uniform(k3, (IN_F, OUT_F), dtype=jnp.float32, minval=-stdv, maxval=stdv)
        t = jnp.ones((1,), dtype=jnp.float32)
        return {'x': x, 'adj': adj, 't': t, 'weight': weight}
    _L2_gnn_all = _L2_gnn_setup()
    _L2_gnn_in = {k: v for k, v in _L2_gnn_all.items() if k in ('t', 'weight')}
    del _L2_gnn_all

    def _L3_gnn_setup():
        import jax, jax.numpy as jnp
        import numpy as np
        EPS = 1e-08
        key = jax.random.key(seed)
        k1, k2, k3, k4 = jax.random.split(key, 4)
        N, IN, OUT = (4096, 256, 256)
        x = jax.random.normal(k1, (N, IN), dtype=jnp.float32)
        adj = jax.random.uniform(k2, (N, N), dtype=jnp.float32)
        W = jax.random.normal(k3, (OUT, IN), dtype=jnp.float32) * (1.0 / np.sqrt(IN))
        b = jax.random.normal(k4, (OUT,), dtype=jnp.float32) * 0.01
        return {'x': x, 'adj': adj, 'W': W, 'b': b}
    _L3_gnn_all = _L3_gnn_setup()
    _L3_gnn_in = {k: v for k, v in _L3_gnn_all.items() if k in ('W', 'b')}
    del _L3_gnn_all
    return {'x': x, 'adj': adj, 'L0_gnn_W_node': _L0_gnn_in['W_node'], 'L0_gnn_b_node': _L0_gnn_in['b_node'], 'L0_gnn_K': _L0_gnn_in['K'], 'L0_gnn_A_self': _L0_gnn_in['A_self'], 'L0_gnn_A_neigh': _L0_gnn_in['A_neigh'], 'L1_gnn_Wq': _L1_gnn_in['Wq'], 'L1_gnn_bq': _L1_gnn_in['bq'], 'L1_gnn_Wk': _L1_gnn_in['Wk'], 'L1_gnn_bk': _L1_gnn_in['bk'], 'L1_gnn_Wv': _L1_gnn_in['Wv'], 'L1_gnn_bv': _L1_gnn_in['bv'], 'L2_gnn_t': _L2_gnn_in['t'], 'L2_gnn_weight': _L2_gnn_in['weight'], 'L3_gnn_W': _L3_gnn_in['W'], 'L3_gnn_b': _L3_gnn_in['b']}

def reference(x, adj, L0_gnn_W_node, L0_gnn_b_node, L0_gnn_K, L0_gnn_A_self, L0_gnn_A_neigh, L1_gnn_Wq, L1_gnn_bq, L1_gnn_Wk, L1_gnn_bk, L1_gnn_Wv, L1_gnn_bv, L2_gnn_t, L2_gnn_weight, L3_gnn_W, L3_gnn_b):
    import jax
    import jax.numpy as jnp

    def _L0_gnn_ref(nodes, adj, W_node, b_node, K, A_self, A_neigh, num_heads):
        import jax, jax.numpy as jnp
        import numpy as np
        N = 2048
        D = 256
        H = 4
        NEG = -10000000000.0
        ALPHA = 0.3
        x = nodes @ W_node + b_node
        feats = jnp.einsum('nd,hdf->hnf', x, K)
        s = jnp.einsum('hnf,hf->hn', feats, A_self) + jnp.einsum('hnf,hf->hn', feats, A_neigh)
        s = jnp.where(s > 0, s, ALPHA * s)
        logits = s[:, :, None] + NEG * (1.0 - adj)[None]
        attn = jax.nn.softmax(logits, axis=-1)
        out = jnp.einsum('hij,hjf->hif', attn, feats)
        out = jnp.mean(out, axis=0)
        return jax.nn.relu(out)

    def _L1_gnn_ref(x, spatial_encoding, edge_encoding, Wq, bq, Wk, bk, Wv, bv):
        import jax, jax.numpy as jnp
        import numpy as np
        N = 4096
        D = 256
        q = x @ Wq.T + bq
        k = x @ Wk.T + bk
        v = x @ Wv.T + bv
        scale = 1.0 / jnp.sqrt(jnp.asarray(q.shape[-1], q.dtype))
        a = q @ k.T * scale + spatial_encoding + edge_encoding
        attn = jax.nn.softmax(a, axis=-1)
        return attn @ v

    def _L2_gnn_ref(x, adj, t, weight):
        import jax, jax.numpy as jnp
        import numpy as np
        N = 5000
        IN_F = 256
        OUT_F = 256
        ts = t[0]
        support = x @ weight
        return (1.0 - ts) * support + ts * (adj @ support)

    def _L3_gnn_ref(x, adj, W, b):
        import jax, jax.numpy as jnp
        import numpy as np
        EPS = 1e-08
        deg = adj.sum(axis=1)
        dis = (deg + EPS) ** (-0.5)
        a_norm = dis[:, None] * adj * dis[None, :]
        h = a_norm @ x
        return h @ W.T + b
    h = jnp.maximum(_layernorm(x, axis=-1), 0.0)
    x = x + _L0_gnn_ref(h, adj, L0_gnn_W_node, L0_gnn_b_node, L0_gnn_K, L0_gnn_A_self, L0_gnn_A_neigh, 4)
    h = jnp.maximum(_layernorm(x, axis=-1), 0.0)
    x = x + _L1_gnn_ref(h, adj, adj, L1_gnn_Wq, L1_gnn_bq, L1_gnn_Wk, L1_gnn_bk, L1_gnn_Wv, L1_gnn_bv)
    h = jnp.maximum(_layernorm(x, axis=-1), 0.0)
    x = x + _L2_gnn_ref(h, adj, L2_gnn_t, L2_gnn_weight)
    h = jnp.maximum(_layernorm(x, axis=-1), 0.0)
    x = x + _L3_gnn_ref(h, adj, L3_gnn_W, L3_gnn_b)
    return x

_drawn_inputs = setup_inputs


def setup_inputs(seed=0):
    import zlib

    import numpy as np

    out = dict(_drawn_inputs(seed))
    spreads = {'L0_gnn_b_node': (0.0, 0.294),
     'L1_gnn_bq': (0.0, 0.8),
     'L1_gnn_bk': (0.0, 0.8),
     'L1_gnn_bv': (0.0, 0.1)}
    factors = {'L1_gnn_Wq': 4.541, 'L1_gnn_Wk': 4.322, 'L3_gnn_b': 8.0}
    for name, (base, spread) in spreads.items():
        noise = np.random.default_rng([zlib.crc32(name.encode()), seed]).standard_normal(out[name].shape)
        drawn = base * np.exp(spread * noise) if base else spread * noise
        out[name] = jnp.asarray(drawn.astype(out[name].dtype))
    for name, factor in factors.items():
        out[name] = (out[name] * factor).astype(out[name].dtype)
    return out
```

```python
from contextlib import ExitStack

import concourse.bass as bass
from concourse import mybir

F32 = mybir.dt.float32
F16 = mybir.dt.float16
ALU = mybir.AluOpType
ACT = mybir.ActivationFunctionType
AX = mybir.AxisListType

P = 128
BANK = 512
NEG = 1.0e10
LN_EPS = 1e-5
DEG_EPS = 1e-8
H_SCALE = 1024.0
T_SCALE = 0.5
LN2_15 = 10.397207708399179
NODE_HEADS = 4


def build(nc, x_in, adj, w_node, b_node, k_heads, wq, bq, wk, wv, bv, t_in, w2, w3, b3, out):
    N, D = x_in.shape
    NB = -(-N // P)
    LAST = N - (NB - 1) * P
    DT = D // P
    CHUNKS = [(c, min(BANK, N - c)) for c in range(0, N, BANK)]
    BPC = BANK // P
    NCH = len(CHUNKS)
    PIECES = [(0, P), (P, BANK - P)] + CHUNKS[1:]
    S_UNIT = H_SCALE * T_SCALE * float(D) ** 0.5
    L0_TURN_Y, L0_FIN, L0_HT = 2, 3, 5
    LOADS = [(0, 5), (5, NB - 1), (NB - 1, NB)]
    assert NCH == 3 and DT == 2 and LAST > 64

    def rows(b):
        return LAST if b == NB - 1 else P

    def cols(b):
        return slice(b * P, b * P + rows(b))

    ctx = ExitStack()
    with ctx:
        def sb(name, shape, dt=F32):
            return ctx.enter_context(nc.sbuf_tensor(name, shape, dt))

        def sem(name):
            return ctx.enter_context(nc.semaphore(name))

        x = sb("x", [P, NB, D])
        h_parts = sb("h_parts", [P, 2, NB, 2, D], F16)
        adj_rows = sb("adj_rows", [P, 3, N])
        adj_scaled = sb("adj_scaled", [P, 2, N])
        adj16 = sb("adj16", [P, 2, N], F16)
        adjT = sb("adjT", [P, NB, N], F16)
        p_hi = sb("p_hi", [P, 2, N], F16)
        p_lo = sb("p_lo", [P, 2, N], F16)
        pT = sb("pT", [P, 2, 2 * NB * P], F16)
        work = sb("work", [P, 4, N])
        logits = work[:, 0:2, :]
        p_f32 = work[:, 2:4, :]
        yT_all = work[:, 0:2, :]
        raw = work[:, :, :].rearrange("p a n -> p (a n)")
        kh_raw = raw[:, 0:DT * NODE_HEADS * D].rearrange("p (h e f) -> p h e f", h=NODE_HEADS, e=DT)
        off = DT * NODE_HEADS * D
        square = {}
        for name in ("w_node", "wq", "wk", "wv", "w3"):
            square[name] = raw[:, off:off + DT * D].rearrange("p (e f) -> p e f", e=DT)
            off += DT * D
        k_sum = raw[:, off:off + DT * D].rearrange("p (e f) -> p e f", e=DT)
        assert off + DT * D <= 4 * N
        hT32 = sb("hT32", [P, DT, N])
        hT = sb("hT", [P, 2, DT, N], F16)
        t32 = sb("t32", [P, DT, BANK])
        tT = sb("tT", [P, 2, DT, N], F16)
        centred = sb("centred", [P, 2, D])
        relu32 = sb("relu32", [P, 2, D])
        y_rows = sb("y_rows", [P, 2, D])
        yT = sb("yT", [P, 2, DT, P])
        head_out = sb("head_out", [P, 2, D])
        wn_T = sb("wn_T", [P, DT, D])
        w_fin = sb("w_fin", [P, 4, DT, D])
        m_qk = sb("m_qk", [P, DT, D])
        mb_qk = sb("mb_qk", [P, DT])
        bnode = sb("bnode", [P, DT])
        bq_col = sb("bq_col", [P, DT])
        bnode_wide = sb("bnode_wide", [P, DT, P])
        bias0 = sb("bias0", [P, D])
        bv_all = sb("bv_all", [P, D])
        b3_all = sb("b3_all", [P, D])
        ts = sb("ts", [P, 1])
        one_minus_t = sb("one_minus_t", [P, 1])
        ident16 = sb("ident16", [P, P], F16)
        ident32 = sb("ident32", [P, P])
        ones = sb("ones", [P, P])
        minus_half = sb("minus_half", [P, NB])
        stats = sb("stats", [P, 4 * NB, 6])
        mean_var = sb("mean_var", [P, 4 * NB, 2])
        var_eps = sb("var_eps", [P, 4 * NB])
        rstd = sb("rstd", [P, 4 * NB])
        rstd3 = sb("rstd3", [P, NB])
        row_max = sb("row_max", [P, 2 * NB])
        shift = sb("shift", [P, 2 * NB])
        den = sb("den", [P, 2 * NB])
        rden = sb("rden", [P, 2 * NB])
        deg = sb("deg", [P, NB])
        deg_eps = sb("deg_eps", [P, NB])
        dis = sb("dis", [P, NB])

        ps = ctx.enter_context(nc.psum_tensor("ps", [P, 8, BANK], F32))
        ps_flat = ps[:, :, :].rearrange("p a b -> p (a b)")
        ps16 = ps_flat.bitcast(F16)
        S_AT, T_AT = 0, 3 * BANK
        ps_adjT = ps16[:, 0:NB * P]
        ps_pT = ps16[:, 2 * T_AT:2 * T_AT + 2 * NB * P]
        ps_y = ps[:, 6, 0:D]
        ps_scores = ps_flat[:, S_AT:S_AT + N]
        ps_yT = ps[:, 7, 0:DT * P].rearrange("p (d r) -> p d r", d=DT)
        ps_big = ps_flat[:, 0:6 * BANK].rearrange("p (d n) -> p d n", d=DT)

        x_loaded = [sem(f"x_loaded{i}") for i in range(3)]
        w_loaded = {n: sem(f"loaded_{n}") for n in ("k", "w_node", "wq", "wk", "wv", "w3", "w2",
                                                    "bnode", "bq", "bv", "b3", "t")}
        adj_loaded = [sem(f"adj_loaded{i}") for i in range(3)]
        ident_ready = sem("ident_ready")
        const_ready = sem("const_ready")
        ksum_ready = sem("ksum_ready")
        bwide_ready = sem("bwide_ready")
        wt_mm = sem("wt_mm")
        wt_ready = sem("wt_ready")
        wprod_mm = sem("wprod_mm")
        wprod_ready = sem("wprod_ready")
        w2_ready = sem("w2_ready")
        omt_ready = sem("omt_ready")
        ps_cleared = sem("ps_cleared")
        stats_ready = sem("stats_ready")
        mv_ready = sem("mv_ready")
        ve0_ready = sem("ve0_ready")
        rstd0_ready = sem("rstd0_ready")
        ve_ready = sem("ve_ready")
        rstd3_ready = sem("rstd3_ready")
        rstd_ready = sem("rstd_ready")
        centred_ready = sem("centred_ready")
        hi_ready = sem("hi_ready")
        relu_ready = sem("relu_ready")
        lo_ready = sem("lo_ready")
        x_added = sem("x_added")
        xb_ready = sem("xb_ready")
        max_ready = sem("max_ready")
        shift_ready = sem("shift_ready")
        exp_ready = sem("exp_ready")
        exp32_ready = sem("exp32_ready")
        plo_ready = sem("plo_ready")
        adj16_ready = sem("adj16_ready")
        adj_scaled_ready = sem("adj_scaled_ready")
        deg_ready = sem("deg_ready")
        dege_ready = sem("dege_ready")
        dis_ready = sem("dis_ready")
        rden_ready = sem("rden_ready")
        p_turned = sem("p_turned")
        pT_ready = sem("pT_ready")
        adj_turned = sem("adj_turned")
        adjT_ready = sem("adjT_ready")
        y_mm = sem("y_mm")
        y_ready = sem("y_ready")
        y_turned = sem("y_turned")
        yT_ready = sem("yT_ready")
        fin_mm = sem("fin_mm")
        head_ready = sem("head_ready")
        hT_mm = sem("hT_mm")
        hT32_ready = sem("hT32_ready")
        hThi_ready = sem("hThi_ready")
        hTlo_ready = sem("hTlo_ready")
        t_mm = sem("t_mm")
        t32_ready = sem("t32_ready")
        tThi_ready = sem("tThi_ready")
        tTlo_ready = sem("tTlo_ready")
        scores_mm = sem("scores_mm")
        logits_ready = max_ready
        big_mm = sem("big_mm")
        big_out = sem("big_out")
        big_out_act = sem("big_out_act")
        stored = sem("stored")

        block = ctx.enter_context(nc.Block())

        def adj_landed(eng, m):
            eng.wait_ge(adj_loaded[m % 3], 16 * (m // 3 + 1))

        def dram_rows(t, b):
            return t[b * P:b * P + rows(b), :]

        @block.sync
        def _(sp):
            def tiles(t):
                return t.rearrange("(e p) f -> p e f", p=P)

            def column(v, e):
                return v[e * P:(e + 1) * P].rearrange("(p a) -> p a", a=1)

            def load_weights_early():
                sp.dma_start(square["w_node"], tiles(w_node)).then_inc(w_loaded["w_node"], 16)
                sp.dma_start(kh_raw.rearrange("p h e f -> p (h e) f"),
                             k_heads.rearrange("h (e p) f -> p (h e) f", p=P)).then_inc(w_loaded["k"], 16)
                for e in range(DT):
                    sp.dma_start(bnode[:, e:e + 1], column(b_node, e)).then_inc(w_loaded["bnode"], 16)

            def load_weights():
                for name, w in (("wv", wv), ("w3", w3), ("wq", wq), ("wk", wk)):
                    sp.dma_start(square[name], tiles(w)).then_inc(w_loaded[name], 16)
                for e in range(DT):
                    sp.dma_start(bq_col[:, e:e + 1], column(bq, e)).then_inc(w_loaded["bq"], 16)
                sp.dma_start(w_fin[:, 2], tiles(w2)).then_inc(w_loaded["w2"], 16)
                for name, to, v, n in (("t", ts, t_in, 1), ("bv", bv_all, bv, D), ("b3", b3_all, b3, D)):
                    sp.dma_start(to[:, :], v.rearrange("(a n) -> a n", a=1).to_broadcast([P, n])
                                 ).then_inc(w_loaded[name], 16)

            for i, (a, z) in enumerate(LOADS[:-1]):
                sp.dma_start(x[:, a:z, :], x_in[a * P:z * P, :].rearrange("(b p) d -> p b d", p=P)
                             ).then_inc(x_loaded[i], 16)
            sp.dma_start(x[0:LAST, NB - 1, :], dram_rows(x_in, NB - 1)).then_inc(x_loaded[2], 16)
            for m in range(2 * NB):
                b = m % NB
                if m >= 3:
                    old = m - 3
                    if old < NB:
                        sp.wait_ge(exp_ready, old + 1)
                        sp.wait_ge(adj16_ready, old + 1)
                    else:
                        sp.wait_ge(adj_scaled_ready, old - NB + 1)
                        sp.wait_ge(deg_ready, old - NB + 1)
                sp.dma_start(adj_rows[0:rows(b), m % 3, :], dram_rows(adj, b)).then_inc(adj_loaded[m % 3], 16)
                if m == 1:
                    load_weights_early()
                if m == 2:
                    load_weights()
            for b in range(NB):
                sp.wait_ge(x_added, 3 * NB + b + 1)
                sp.dma_start(dram_rows(out, b), x[0:rows(b), b, :]).then_inc(stored, 16)
            sp.wait_ge(stored, 16 * NB)

        @block.gpsimd
        def _(pool):
            g = nc.gpsimd
            g.memset(ident16[:, :], 0.0).then_inc(ident_ready, 1)
            g.memset(ident32[:, :], 0.0).then_inc(ident_ready, 1)
            g.memset(minus_half[:, :], -0.5).then_inc(const_ready, 1)
            g.memset(ones[:, :], 1.0).then_inc(const_ready, 1)
            pool.wait_ge(ident_ready, 2)
            for m in (ident16, ident32):
                g.affine_select(out=m[:, :], in_=m[:, :], compare_op=ALU.not_equal, fill=1.0, base=0,
                                pattern=[[-1, P]], channel_multiplier=1).then_inc(ident_ready, 1)
            pool.wait_ge(const_ready, 2)

            def ln_scale(n):
                layer, b = divmod(n, NB)
                r = rows(b)
                pool.wait_ge(mv_ready, n + 1)
                g.tensor_scalar(var_eps[0:r, n:n + 1], mean_var[0:r, n, 1:2], H_SCALE ** -2, LN_EPS * H_SCALE ** -2,
                                ALU.mult, ALU.add).then_inc(ve_ready, 1)
                pool.wait_ge(ve_ready, n - NB + 1)
                if layer < 3:
                    g.tensor_tensor(rstd[0:r, n:n + 1], var_eps[0:r, n:n + 1], minus_half[0:r, 0:1],
                                    ALU.pow).then_inc(rstd_ready, 1)
                    return
                g.tensor_tensor(rstd3[0:r, b:b + 1], var_eps[0:r, n:n + 1], minus_half[0:r, 0:1],
                                ALU.pow).then_inc(rstd3_ready, 1)
                pool.wait_ge(rstd3_ready, b + 1)
                pool.wait_ge(dis_ready, b + 1)
                g.tensor_tensor(rstd[0:r, n:n + 1], rstd3[0:r, b:b + 1], dis[0:r, b:b + 1],
                                ALU.mult).then_inc(rstd_ready, 1)

            def ln_lo(n):
                layer, b = divmod(n, NB)
                r = rows(b)
                pool.wait_ge(relu_ready, n + 1)
                pool.wait_ge(hi_ready, n + 1)
                if layer >= 2:
                    pool.wait_ge(y_mm, NB * (layer - 1))
                g.tensor_tensor(h_parts[0:r, layer % 2, b, 1, :], relu32[0:r, n % 2, :],
                                h_parts[0:r, layer % 2, b, 0, :], ALU.subtract).then_inc(lo_ready, 1)

            def cast_adj(b):
                adj_landed(pool, b)
                if b >= 2:
                    pool.wait_ge(adj_turned, b - 1)
                g.tensor_scalar(adj16[0:rows(b), b % 2, :], adj_rows[0:rows(b), b % 3, :], 1.0, 1.0,
                                ALU.mult, ALU.mult).then_inc(adj16_ready, 1)

            def split_hT(b):
                pool.wait_ge(hT32_ready, b + 1)
                g.tensor_scalar(hT[:, 0, :, cols(b)], hT32[:, :, cols(b)], 1.0, 1.0,
                                ALU.mult, ALU.mult).then_inc(hThi_ready, 1)
                pool.wait_ge(hThi_ready, b + 1)
                g.tensor_tensor(hT[:, 1, :, cols(b)], hT32[:, :, cols(b)], hT[:, 0, :, cols(b)],
                                ALU.subtract).then_inc(hTlo_ready, 1)

            def split_t(c):
                a, w = CHUNKS[c]
                pool.wait_ge(t32_ready, 2 * c + 2)
                g.tensor_scalar(tT[:, 0, :, a:a + w], t32[:, :, 0:w], 1.0, 1.0,
                                ALU.mult, ALU.mult).then_inc(tThi_ready, 1)
                pool.wait_ge(tThi_ready, c + 1)
                g.tensor_tensor(tT[:, 1, :, a:a + w], t32[:, :, 0:w], tT[:, 0, :, a:a + w],
                                ALU.subtract).then_inc(tTlo_ready, 1)

            def prepare_weights():
                pool.wait_ge(w_loaded["k"], 16)
                g.tensor_tensor(k_sum, kh_raw[:, 0], kh_raw[:, 1], ALU.add).then_inc(ksum_ready, 1)
                g.tensor_tensor(kh_raw[:, 2], kh_raw[:, 2], kh_raw[:, 3], ALU.add).then_inc(ksum_ready, 1)
                pool.wait_ge(ksum_ready, 2)
                g.tensor_tensor(k_sum, k_sum, kh_raw[:, 2], ALU.add).then_inc(ksum_ready, 1)
                pool.wait_ge(ksum_ready, 3)
                g.tensor_scalar(k_sum, k_sum, 1.0 / NODE_HEADS, 1.0 / H_SCALE, ALU.mult, ALU.mult
                                ).then_inc(ksum_ready, 1)
                pool.wait_ge(w_loaded["bnode"], 16 * DT)
                for e in range(DT):
                    g.tensor_scalar(bnode_wide[:, e, :], ones[:, :], bnode[:, e:e + 1], H_SCALE,
                                    ALU.mult, ALU.mult).then_inc(bwide_ready, 1)
                pool.wait_ge(w_loaded["t"], 16)
                g.tensor_scalar(one_minus_t[:, :], ts[:, :], -1.0, 1.0, ALU.mult, ALU.add).then_inc(omt_ready, 1)

            for k, (a, z) in enumerate(LOADS):
                r = rows(a)
                pool.wait_ge(mv_ready, z)
                g.tensor_scalar(var_eps[0:r, a:z], mean_var[0:r, a:z, 1], H_SCALE ** -2, LN_EPS * H_SCALE ** -2,
                                ALU.mult, ALU.add).then_inc(ve0_ready, 1)
                pool.wait_ge(ve0_ready, k + 1)
                g.tensor_tensor(rstd[0:r, a:z], var_eps[0:r, a:z], minus_half[0:r, 0:z - a], ALU.pow
                                ).then_inc(rstd0_ready, 1)
            ln_lo(0)
            ln_lo(1)
            cast_adj(0)
            for b in range(2, NB):
                ln_lo(b)
            cast_adj(1)
            prepare_weights()
            for s in range(NB + L0_HT + 1):
                if 0 <= s - L0_FIN < NB:
                    ln_scale(NB + s - L0_FIN)
                if 1 <= s and s + 1 < NB:
                    cast_adj(s + 1)
                if 0 <= s - L0_FIN - 1 < NB:
                    ln_lo(NB + s - L0_FIN - 1)
                b = s - L0_HT
                if 0 <= b < NB:
                    split_hT(b)
                    if b % BPC == BPC - 1 or b == NB - 1:
                        split_t(b // BPC)

            def scale_adj(b):
                adj_landed(pool, NB + b)
                if b >= 2:
                    pool.wait_ge(logits_ready, NB + b - 1)
                g.tensor_scalar(adj_scaled[0:rows(b), b % 2, :], adj_rows[0:rows(b), (NB + b) % 3, :],
                                2.0, S_UNIT, ALU.mult, ALU.mult).then_inc(adj_scaled_ready, 1)

            def add_bias(layer, b, bias):
                r = rows(b)
                pool.wait_ge(centred_ready, layer * NB + b + 1)
                g.tensor_tensor(x[0:r, b, :], x[0:r, b, :], bias[0:r, :], ALU.add).then_inc(xb_ready, 1)

            pool.wait_ge(w_loaded["bv"], 16)
            pool.wait_ge(x_added, NB)
            scale_adj(0)
            for s in range(NB + 4):
                if 0 <= s - 4 < NB:
                    ln_scale(2 * NB + s - 4)
                if s + 1 < NB:
                    scale_adj(s + 1)
                if 0 <= s - 4 < NB:
                    ln_lo(2 * NB + s - 4)
                if s < NB:
                    add_bias(1, s, bv_all)
            for b in range(NB):
                r = rows(b)
                pool.wait_ge(deg_ready, b + 1)
                g.tensor_scalar(deg_eps[0:r, b:b + 1], deg[0:r, b:b + 1], 1.0, DEG_EPS, ALU.mult, ALU.add
                                ).then_inc(dege_ready, 1)
                pool.wait_ge(dege_ready, b + 1)
                g.tensor_tensor(dis[0:r, b:b + 1], deg_eps[0:r, b:b + 1], minus_half[0:r, 0:1], ALU.pow
                                ).then_inc(dis_ready, 1)
            pool.wait_ge(w_loaded["b3"], 16)
            for b in range(NB + 1):
                if b < NB:
                    ln_scale(3 * NB + b)
                if b:
                    ln_lo(3 * NB + b - 1)
            for b in range(NB):
                add_bias(3, b, b3_all)

        @block.scalar
        def _(act):
            s_ = nc.scalar

            def ln_relu(n):
                layer, b = divmod(n, NB)
                r = rows(b)
                act.wait_ge(centred_ready, n + 1)
                if layer >= 2:
                    act.wait_ge(y_mm, NB * (layer - 1))
                if n >= 2:
                    act.wait_ge(lo_ready, n - 1)
                s_.activation(h_parts[0:r, layer % 2, b, 0, :], centred[0:r, n % 2, :], ACT.Relu
                              ).then_inc(hi_ready, 1)
                s_.activation(relu32[0:r, n % 2, :], centred[0:r, n % 2, :], ACT.Relu).then_inc(relu_ready, 1)

            def exp0(b):
                r = rows(b)
                act.wait_ge(shift_ready, b + 1)
                adj_landed(act, b)
                if b >= 2:
                    act.wait_ge(p_turned, b - 1)
                s_.activation(p_hi[0:r, b % 2, :], adj_rows[0:r, b % 3, :], ACT.Exp, bias=shift[0:r, b:b + 1],
                              scale=NEG, accum_out=den[0:r, b:b + 1]).then_inc(exp_ready, 1)

            def out_adjT(b):
                act.wait_ge(adj_turned, b + 1)
                s_.activation(adjT[:, :, cols(b)],
                              ps_adjT.rearrange("p (j i) -> p j i", j=NB)[:, :, 0:rows(b)], ACT.Copy
                              ).then_inc(adjT_ready, 1)

            def out_y(n):
                r = rows(n % NB)
                act.wait_ge(y_mm, n + 1)
                act.wait_ge(rden_ready, n + 1)
                if n >= 2:
                    act.wait_ge(y_turned, n - 1)
                s_.activation(y_rows[0:r, n % 2, :], ps_y[0:r, :], ACT.Copy, scale=rden[0:r, n:n + 1]
                              ).then_inc(y_ready, 1)

            def out_yT(n):
                r = rows(n % NB)
                act.wait_ge(y_turned, n + 1)
                if n >= 2:
                    act.wait_ge(fin_mm, n - 1)
                s_.activation(yT[:, n % 2, :, 0:r], ps_yT[:, :, 0:r], ACT.Copy).then_inc(yT_ready, 1)

            def out_hT(b):
                act.wait_ge(hT_mm, b + 1)
                s_.activation(hT32[:, :, cols(b)], ps[:, 2, 0:DT * P].rearrange("p (d r) -> p d r", d=DT)[:, :, 0:rows(b)],
                              ACT.Copy).then_inc(hT32_ready, 1)

            def out_t(c):
                a, w = CHUNKS[c]
                for d in range(DT):
                    act.wait_ge(t_mm, DT * c + d + 1)
                    if c:
                        act.wait_ge(tTlo_ready, c)
                    s_.activation(t32[:, d, 0:w], ps[:, (2, 5)[d], 0:w], ACT.Identity, bias=mb_qk[:, d:d + 1],
                                  scale=T_SCALE / H_SCALE).then_inc(t32_ready, 1)

            def out_weight(to, bank, done, count, ready, scale=1.0):
                act.wait_ge(done, count)
                s_.activation(to, ps[:, bank, :].rearrange("p (e f) -> p e f", e=DT), ACT.Copy, scale=scale
                              ).then_inc(ready, 1)

            def out_weights(s):
                if s == 0:
                    out_weight(wn_T[:, :, :], 5, wt_mm, 1, wt_ready)
                if s == 1:
                    out_weight(w_fin[:, 0], 5, wprod_mm, 1, wprod_ready)
                    act.wait_ge(wprod_mm, 2)
                    s_.activation(bias0[:, :], ps[:, 7, 0:D], ACT.Copy).then_inc(wprod_ready, 1)
                if s == 2:
                    out_weight(w_fin[:, 1], 2, wt_mm, 2, wt_ready, 1.0 / H_SCALE)
                if s == 3:
                    out_weight(w_fin[:, 3], 2, wt_mm, 3, wt_ready, 1.0 / H_SCALE)
                    out_weight(m_qk[:, :, :], 2, wprod_mm, 3, wprod_ready)
                if s == 4:
                    act.wait_ge(wprod_mm, 4)
                    s_.activation(mb_qk[:, :], ps[:, 2, 0:DT], ACT.Copy, scale=T_SCALE).then_inc(wprod_ready, 1)
                    act.wait_ge(w_loaded["w2"], 16)
                    s_.activation(w_fin[:, 2], w_fin[:, 2], ACT.Copy, scale=1.0 / H_SCALE).then_inc(w2_ready, 1)

            for b in range(NB):
                ln_relu(b)
            exp0(0)
            for s in range(NB + L0_HT + 1):
                if 0 <= s - L0_TURN_Y < NB:
                    out_y(s - L0_TURN_Y)
                if s + 1 < NB:
                    exp0(s + 1)
                if s < NB:
                    out_adjT(s)
                out_weights(s)
                if 0 <= s - L0_TURN_Y < NB:
                    out_yT(s - L0_TURN_Y)
                if 0 <= s - L0_FIN - 1 < NB:
                    ln_relu(NB + s - L0_FIN - 1)
                b = s - L0_HT
                if 0 <= b < NB:
                    out_hT(b)
                    if b % BPC == BPC - 1 or b == NB - 1:
                        out_t(b // BPC)

            def degree(b):
                r = rows(b)
                adj_landed(act, NB + b)
                if b:
                    act.wait_ge(deg_ready, b)
                s_.activation(adj16[0:r, b % 2, :], adj_rows[0:r, (NB + b) % 3, :], ACT.Copy,
                              accum_out=deg[0:r, b:b + 1]).then_inc(deg_ready, 1)

            def exp1(b):
                r = rows(b)
                n = NB + b
                act.wait_ge(shift_ready, n + 1)
                if b >= 2:
                    act.wait_ge(plo_ready, b - 1)
                s_.activation(p_f32[0:r, b % 2, :], logits[0:r, b % 2, :], ACT.Exp, bias=shift[0:r, n:n + 1],
                              accum_out=den[0:r, n:n + 1]).then_inc(exp32_ready, 1)
                if b >= 2:
                    act.wait_ge(p_turned, n - 1)
                s_.activation(p_hi[0:r, b % 2, :], logits[0:r, b % 2, :], ACT.Exp, bias=shift[0:r, n:n + 1]
                              ).then_inc(exp_ready, 1)

            for s in range(NB + 4):
                if 0 <= s - 3 < NB:
                    out_y(NB + s - 3)
                if 0 <= s - 4 < NB:
                    ln_relu(2 * NB + s - 4)
                if s < NB:
                    degree(s)
                if 0 <= s - 3 < NB:
                    out_yT(NB + s - 3)
                if s < NB:
                    exp1(s)
            act.wait_ge(omt_ready, 1)
            for b in range(NB):
                act.wait_ge(hT_mm, NB + b + 1)
                s_.activation(hT32[:, :, cols(b)], ps_yT[:, :, 0:rows(b)], ACT.Copy, scale=one_minus_t[:, 0:1]
                              ).then_inc(hT32_ready, 1)
            for b in range(NB):
                ln_relu(3 * NB + b)
            act.wait_ge(big_mm, 2)
            for a, w in PIECES:
                s_.activation(yT_all[:, 1, a:a + w], ps_big[:, 1, a:a + w], ACT.Copy).then_inc(big_out_act, 1)

        @block.vector
        def _(dve):
            v = nc.vector

            def ln_stats(n):
                layer, b = divmod(n, NB)
                r = rows(b)
                if layer == 0:
                    dve.wait_ge(x_loaded[[k for k, (a, z) in enumerate(LOADS) if a <= b < z][0]], 16)
                else:
                    dve.wait_ge(x_added, n - NB + 1)
                v.bn_stats(stats[0:r, n, :], x[0:r, b, :]).then_inc(stats_ready, 1)
                dve.wait_ge(stats_ready, n + 1)
                v.bn_aggr(mean_var[0:r, n, :], stats[0:r, n, :]).then_inc(mv_ready, 1)

            def ln_centre(n):
                layer, b = divmod(n, NB)
                r = rows(b)
                if layer == 0:
                    dve.wait_ge(rstd0_ready, [k for k, (a, z) in enumerate(LOADS) if a <= b < z][0] + 1)
                else:
                    dve.wait_ge(rstd_ready, n - NB + 1)
                if n >= 2:
                    dve.wait_ge(relu_ready, n - 1)
                v.tensor_scalar(centred[0:r, n % 2, :], x[0:r, b, :], mean_var[0:r, n, 0:1], rstd[0:r, n:n + 1],
                                ALU.subtract, ALU.mult).then_inc(centred_ready, 1)

            def max0(b):
                r = rows(b)
                adj_landed(dve, b)
                v.tensor_reduce(row_max[0:r, b:b + 1], adj_rows[0:r, b % 3, :], AX.X, ALU.max).then_inc(max_ready, 1)
                dve.wait_ge(max_ready, b + 1)
                v.tensor_scalar(shift[0:r, b:b + 1], row_max[0:r, b:b + 1], -NEG, None, ALU.mult
                                ).then_inc(shift_ready, 1)

            def out_pT(n):
                layer, b = divmod(n, NB)
                w = (1 + layer) * NB
                dve.wait_ge(p_turned, n + 1)
                if n >= 2:
                    dve.wait_ge(y_mm, n - 1)
                v.tensor_copy(pT[:, n % 2, 0:w * P].rearrange("p (j i) -> p j i", j=w)[:, :, 0:rows(b)],
                              ps_pT[:, 0:w * P].rearrange("p (j i) -> p j i", j=w)[:, :, 0:rows(b)]
                              ).then_inc(pT_ready, 1)

            def inverse(n):
                r = rows(n % NB)
                dve.wait_ge(exp_ready, n + 1)
                v.reciprocal(rden[0:r, n:n + 1], den[0:r, n:n + 1]).then_inc(rden_ready, 1)

            def add0(b):
                r = rows(b)
                dve.wait_ge(fin_mm, b + 1)
                if b == 0:
                    dve.wait_ge(wprod_ready, 2)
                if b >= 2:
                    dve.wait_ge(x_added, b - 1)
                v.tensor_tensor(head_out[0:r, b % 2, :], ps[0:r, 5, 0:D], bias0[0:r, :], ALU.add
                                ).then_inc(head_ready, 1)
                dve.wait_ge(head_ready, b + 1)
                v.scalar_tensor_tensor(out=x[0:r, b, :], in0=head_out[0:r, b % 2, :], scalar=0.0, in1=x[0:r, b, :],
                                       op0=ALU.max, op1=ALU.add).then_inc(x_added, 1)

            for at in (S_AT, T_AT):
                v.memset(ps_flat[:, at + (NB - 1) * P // 2:at + NB * P // 2], 0.0).then_inc(ps_cleared, 1)
            for b in range(NB):
                ln_stats(b)
            for b in range(NB):
                ln_centre(b)
            max0(0)
            for s in range(NB + L0_FIN + 1):
                if s + 1 < NB:
                    max0(s + 1)
                if 0 <= s - L0_FIN < NB:
                    add0(s - L0_FIN)
                    ln_stats(NB + s - L0_FIN)
                if s < NB:
                    inverse(s)
                    out_pT(s)
                if 0 <= s - L0_FIN < NB:
                    ln_centre(NB + s - L0_FIN)

            def logits_max(b):
                r = rows(b)
                n = NB + b
                dve.wait_ge(scores_mm, b + 1)
                dve.wait_ge(adj_scaled_ready, b + 1)
                if b >= 2:
                    dve.wait_ge(exp_ready, n - 1)
                v.tensor_tensor_reduce(logits[0:r, b % 2, :], ps_scores[0:r, :], adj_scaled[0:r, b % 2, :],
                                       1.0 / S_UNIT, -3.0e38, ALU.add, ALU.max, row_max[0:r, n:n + 1]
                                       ).then_inc(max_ready, 1)
                dve.wait_ge(max_ready, n + 1)
                v.tensor_scalar(shift[0:r, n:n + 1], row_max[0:r, n:n + 1], -1.0, LN2_15, ALU.mult, ALU.add
                                ).then_inc(shift_ready, 1)

            def p_low(b):
                r = rows(b)
                n = NB + b
                dve.wait_ge(exp_ready, n + 1)
                if b >= 2:
                    dve.wait_ge(p_turned, n - 1)
                v.tensor_tensor(p_lo[0:r, b % 2, :], p_f32[0:r, b % 2, :], p_hi[0:r, b % 2, :], ALU.subtract
                                ).then_inc(plo_ready, 1)

            def add1(b):
                r = rows(b)
                dve.wait_ge(fin_mm, NB + b + 1)
                dve.wait_ge(xb_ready, b + 1)
                v.tensor_tensor(x[0:r, b, :], ps[0:r, 7, 0:D], x[0:r, b, :], ALU.add).then_inc(x_added, 1)

            dve.wait_ge(t32_ready, DT * NCH)
            v.memset(ps_flat[:, T_AT + (2 * NB - 1) * P // 2:T_AT + NB * P], 0.0).then_inc(ps_cleared, 1)
            for s in range(NB + 4):
                if 0 <= s - 4 < NB:
                    add1(s - 4)
                    ln_stats(2 * NB + s - 4)
                    ln_centre(2 * NB + s - 4)
                if s < NB:
                    logits_max(s)
                if 0 <= s - 1 < NB:
                    out_pT(NB + s - 1)
                if s < NB:
                    p_low(s)
                    inverse(NB + s)

            dve.wait_ge(w_loaded["t"], 16)
            dve.wait_ge(big_mm, 1)
            dve.wait_ge(hT32_ready, 2 * NB)
            for a, w in PIECES:
                v.scalar_tensor_tensor(out=yT_all[:, :, a:a + w], in0=ps_big[:, :, a:a + w], scalar=ts[:, 0:1],
                                       in1=hT32[:, :, a:a + w], op0=ALU.mult, op1=ALU.add).then_inc(big_out, 1)
            for b in range(NB):
                r = rows(b)
                dve.wait_ge(fin_mm, 2 * NB + b + 1)
                v.tensor_tensor(x[0:r, b, :], ps[0:r, 6 + b % 2, 0:D], x[0:r, b, :], ALU.add).then_inc(x_added, 1)
                if b >= 2:
                    ln_centre(3 * NB + b - 2)
                ln_stats(3 * NB + b)
            ln_centre(4 * NB - 2)
            ln_centre(4 * NB - 1)
            dve.wait_ge(big_mm, 2)
            for a, w in PIECES:
                v.tensor_copy(yT_all[:, 0, a:a + w], ps_big[:, 0, a:a + w]).then_inc(big_out, 1)
            for b in range(NB):
                r = rows(b)
                dve.wait_ge(fin_mm, 3 * NB + b + 1)
                dve.wait_ge(xb_ready, NB + b + 1)
                v.scalar_tensor_tensor(out=x[0:r, b, :], in0=ps[0:r, 6 + b % 2, 0:D], scalar=dis[0:r, b:b + 1],
                                       in1=x[0:r, b, :], op0=ALU.mult, op1=ALU.add).then_inc(x_added, 1)

        @block.tensor
        def _(pe):
            t = nc.tensor
            def turn_weight(name, bank):
                pe.wait_ge(w_loaded[name], 16)
                for e in range(DT):
                    for d in range(DT):
                        last = t.transpose(ps[:, bank, e * D + d * P:e * D + (d + 1) * P],
                                           square[name][:, d, e * P:(e + 1) * P], ident32[:, :])
                last.then_inc(wt_mm, 1)

            def product(out_of, lhs, rhs):
                for m, o in enumerate(out_of):
                    for e in range(DT):
                        last = t.matmul(o, lhs(e, m), rhs(e), start=(e == 0), stop=(e == DT - 1))
                last.then_inc(wprod_mm, 1)

            def tile_of(w):
                return lambda e, m: w[:, e, m * P:(m + 1) * P]

            def prepare_weights(s):
                if s == 0:
                    turn_weight("w_node", 5)
                if s == 1:
                    pe.wait_ge(wt_ready, 1)
                    pe.wait_ge(ksum_ready, 4)
                    product([ps[:, 5, d * D:(d + 1) * D] for d in range(DT)], tile_of(wn_T), lambda e: k_sum[:, e, :])
                    pe.wait_ge(bwide_ready, DT)
                    product([ps[:, 7, 0:D]], lambda e, m: bnode_wide[:, e, :], lambda e: k_sum[:, e, :])
                if s == 2:
                    turn_weight("wv", 2)
                if s == 3:
                    pe.wait_ge(wt_ready, 2)
                    turn_weight("w3", 2)
                    pe.wait_ge(wt_ready, 3)
                    pe.wait_ge(w_loaded["wq"], 16)
                    pe.wait_ge(w_loaded["wk"], 16)
                    product([ps[:, 2, d * D:(d + 1) * D] for d in range(DT)], tile_of(square["wq"]),
                            lambda e: square["wk"][:, e, :])
                if s == 4:
                    pe.wait_ge(wprod_ready, 3)
                    pe.wait_ge(w_loaded["bq"], 16 * DT)
                    product([ps[:, 2, d:d + 1] for d in range(DT)], tile_of(square["wk"]),
                            lambda e: bq_col[:, e:e + 1])

            def turn(dst, src, b, at):
                r = rows(b)
                for j in range(NB):
                    last = t.transpose(dst[0:rows(j), (at + j) * P:(at + j) * P + r], src[0:r, cols(j)],
                                       ident16[0:r, 0:r])
                return last

            def turn0(b):
                if b:
                    pe.wait_ge(pT_ready, b)
                    pe.wait_ge(adjT_ready, b)
                pe.wait_ge(exp_ready, b + 1)
                turn(ps_pT, p_hi[:, b % 2, :], b, 0).then_inc(p_turned, 1)
                pe.wait_ge(adj16_ready, b + 1)
                turn(ps_adjT, adj16[:, b % 2, :], b, 0).then_inc(adj_turned, 1)

            def weigh(n):
                layer, b = divmod(n, NB)
                r = rows(b)
                pe.wait_ge(pT_ready, n + 1)
                if n:
                    pe.wait_ge(y_ready, n)
                if b == 0:
                    pe.wait_ge(lo_ready, (layer + 1) * NB)
                terms = [(0, 0), (0, 1)] + [(1, 0)] * layer
                for j in range(NB):
                    for k, (pp, hp) in enumerate(terms):
                        tile = pT[0:rows(j), n % 2, (pp * NB + j) * P:(pp * NB + j) * P + r]
                        last = t.matmul(ps_y[0:r, :], tile, h_parts[0:rows(j), layer % 2, j, hp, :],
                                        start=(j == 0 and k == 0), stop=(j == NB - 1 and k == len(terms) - 1))
                last.then_inc(y_mm, 1)

            def turn_y(n):
                r = rows(n % NB)
                pe.wait_ge(y_ready, n + 1)
                if n >= NB + 1:
                    pe.wait_ge(x_added, n)
                elif n:
                    pe.wait_ge(yT_ready, n)
                else:
                    pe.wait_ge(wprod_ready, 2)
                for d in range(DT):
                    last = t.transpose(ps_yT[:, d, 0:r], y_rows[0:r, n % 2, d * P:(d + 1) * P], ident32[0:r, 0:r])
                last.then_inc(y_turned, 1)

            def final(n, bank, left):
                layer, b = divmod(n, NB)
                r = rows(b)
                for d in range(DT):
                    last = t.matmul(ps[0:r, bank, 0:D], left(d), w_fin[:, layer, d, :],
                                    start=(d == 0), stop=(d == DT - 1))
                last.then_inc(fin_mm, 1)

            def final_att(n, bank):
                pe.wait_ge(yT_ready, n + 1)
                if bank == 5 and n:
                    pe.wait_ge(head_ready, n)
                    if (n - 1 - L0_HT + L0_FIN) >= BPC - 1:
                        pe.wait_ge(t32_ready, DT * ((n - L0_HT + L0_FIN) // BPC))
                final(n, bank, lambda d: yT[:, n % 2, d, 0:rows(n % NB)])

            def turn_h(n, bank):
                layer, b = divmod(n, NB)
                r = rows(b)
                pe.wait_ge(lo_ready, n + 1)
                for d in range(DT):
                    for part in range(2):
                        last = t.matmul(ps[:, bank, d * P:d * P + r],
                                        h_parts[0:r, layer % 2, b, part, d * P:(d + 1) * P],
                                        ident16[0:r, 0:r], start=(part == 0), stop=(part == 1))
                last.then_inc(hT_mm, 1)

            def make_t(c):
                a, w = CHUNKS[c]
                last_block = min((c + 1) * BPC, NB)
                pe.wait_ge(hT32_ready, last_block)
                pe.wait_ge(head_ready, min(last_block + L0_HT - L0_FIN, NB))
                for m, bank in enumerate((2, 5)):
                    for d in range(DT):
                        last = t.matmul(ps[:, bank, 0:w], m_qk[:, d, m * P:(m + 1) * P], hT32[:, d, a:a + w],
                                        start=(d == 0), stop=(d == DT - 1))
                    last.then_inc(t_mm, 1)

            pe.wait_ge(ident_ready, 4)
            pe.wait_ge(ps_cleared, 2)
            for s in range(NB + L0_HT + 1):
                if 0 <= s - L0_FIN < NB:
                    final_att(s - L0_FIN, 5)
                if s < NB:
                    turn0(s)
                prepare_weights(s)
                if 0 <= s - L0_TURN_Y < NB:
                    turn_y(s - L0_TURN_Y)
                if 0 <= s - 1 < NB:
                    weigh(s - 1)
                b = s - L0_HT
                if 0 <= b < NB:
                    if b == 0:
                        pe.wait_ge(wprod_ready, 4)
                    else:
                        pe.wait_ge(hT32_ready, b)
                        if b % BPC == 0:
                            pe.wait_ge(t32_ready, 2 * (b // BPC))
                    turn_h(NB + b, 2)
                    if b % BPC == BPC - 1 or b == NB - 1:
                        make_t(b // BPC)

            def scores(b):
                r = rows(b)
                if b:
                    pe.wait_ge(logits_ready, NB + b)
                else:
                    pe.wait_ge(hTlo_ready, NB)
                    pe.wait_ge(adjT_ready, NB)
                    pe.wait_ge(t32_ready, 2 * NCH)
                pe.wait_ge(tTlo_ready, b // BPC + 1)
                for c, (a, w) in enumerate(CHUNKS):
                    terms = [(d, tp, hp) for d in range(DT) for tp, hp in ((0, 0), (0, 1), (1, 0))]
                    for k, (d, tp, hp) in enumerate(terms):
                        last = t.matmul(ps[0:r, c, 0:w], tT[:, tp, d, cols(b)], hT[:, hp, d, a:a + w],
                                        start=(k == 0), stop=(k == len(terms) - 1))
                last.then_inc(scores_mm, 1)

            def turn1(b):
                n = NB + b
                pe.wait_ge(pT_ready, n)
                pe.wait_ge(exp_ready, n + 1)
                if b == 0:
                    pe.wait_ge(ps_cleared, 3)
                turn(ps_pT, p_hi[:, b % 2, :], b, 0)
                pe.wait_ge(plo_ready, b + 1)
                turn(ps_pT, p_lo[:, b % 2, :], b, NB).then_inc(p_turned, 1)

            for s in range(NB + 4):
                if 0 <= s - 4 < NB:
                    final_att(NB + s - 4, 7)
                if s < NB:
                    scores(s)
                if 0 <= s - 1 < NB:
                    turn1(s - 1)
                if 0 <= s - 3 < NB:
                    turn_y(NB + s - 3)
                if 0 <= s - 2 < NB:
                    weigh(NB + s - 2)

            def gather(layer, j, first, last_one, r=P):
                par = layer % 2
                for d in range(DT):
                    for part in range(2):
                        left = h_parts[0:r, par, j, part, d * P:(d + 1) * P]
                        for a, w in CHUNKS:
                            last = t.matmul(ps_big[:, d, a:a + w], left, adjT[0:r, j, a:a + w],
                                            start=(first and part == 0), stop=(last_one and part == 1))
                return last

            pe.wait_ge(x_added, 2 * NB)
            pe.wait_ge(pT_ready, 2 * NB)
            for j in range(NB):
                if j:
                    pe.wait_ge(hT32_ready, NB + j)
                turn_h(2 * NB + j, 7)
                last = gather(2, j, j == 0, j == NB - 1, rows(j))
            last.then_inc(big_mm, 1)

            def final_big(layer, b):
                piece = [k for k, (a, w) in enumerate(PIECES) if a <= b * P < a + w][0]
                pe.wait_ge(big_out, (layer - 2) * len(PIECES) + piece + 1)
                if layer == 3:
                    pe.wait_ge(big_out_act, piece + 1)
                elif b == 0:
                    pe.wait_ge(w2_ready, 1)
                if b >= 2:
                    pe.wait_ge(x_added, layer * NB + b - 1)
                final(layer * NB + b, 6 + b % 2, lambda d: yT_all[:, d, cols(b)])

            nxt = 5
            for b in range(nxt):
                final_big(2, b)
            pe.wait_ge(big_out, len(PIECES))
            for j in range(NB):
                pe.wait_ge(lo_ready, 3 * NB + j + 1)
                last = gather(3, j, j == 0, j == NB - 1, rows(j))
                for b in range(nxt, min(nxt + 2, NB)):
                    final_big(2, b)
                nxt += 2
            last.then_inc(big_mm, 1)
            pe.wait_ge(x_added, 3 * NB)
            for b in range(NB):
                final_big(3, b)


INS = ["x", "adj", "L0_gnn_W_node", "L0_gnn_b_node", "L0_gnn_K", "L1_gnn_Wq", "L1_gnn_bq", "L1_gnn_Wk",
       "L1_gnn_Wv", "L1_gnn_bv", "L2_gnn_t", "L2_gnn_weight", "L3_gnn_W", "L3_gnn_b"]


def kernel(**inputs):
    import numpy as np
    import concourse.bacc as bacc
    from concourse.bass_utils import run_bass_kernel_spmd

    nc = bacc.Bacc("TRN2", target_bir_lowering=False, num_devices=1)
    arrays, args = {}, []
    for name in INS:
        a = np.ascontiguousarray(inputs[name])
        arrays[f"in_{name}"] = a
        args.append(nc.dram_tensor(f"in_{name}", a.shape, mybir.dt.from_np(a.dtype), kind="ExternalInput").ap())
    args.append(nc.dram_tensor("out_x", inputs["x"].shape, F32, kind="ExternalOutput").ap())
    build(nc, *args)
    r = run_bass_kernel_spmd(nc, [arrays], core_ids=[0])
    return r.results[0]["out_x"]
```

```python
from contextlib import ExitStack

import concourse.bass as bass
from concourse import mybir

F32 = mybir.dt.float32
F16 = mybir.dt.float16
ALU = mybir.AluOpType
ACT = mybir.ActivationFunctionType
AX = mybir.AxisListType

P = 128
BANK = 512
NEG = 1.0e10
LN_EPS = 1e-5
DEG_EPS = 1e-8
H_SCALE = 1024.0
T_SCALE = 0.5
LN2_15 = 10.397207708399179
NODE_HEADS = 4


def build(nc, x_in, adj, w_node, b_node, k_heads, wq, bq, wk, wv, bv, t_in, w2, w3, b3, out):
    N, D = x_in.shape
    NB = -(-N // P)
    LAST = N - (NB - 1) * P
    DT = D // P
    CHUNKS = [(c, min(BANK, N - c)) for c in range(0, N, BANK)]
    BPC = BANK // P
    NCH = len(CHUNKS)
    S_UNIT = H_SCALE * T_SCALE * float(D) ** 0.5
    L0_TURN_Y, L0_FIN, L0_HT = 2, 3, 5
    T_STEP = BPC + L0_HT
    T_BANKS = [(2, 5)] + [(6, 7)] * (NCH - 1)
    LOADS = [(0, 5), (5, NB - 1), (NB - 1, NB)]
    RING = 6
    assert NCH == 3 and DT == 2 and LAST > 64

    def rows(b):
        return LAST if b == NB - 1 else P

    def cols(b):
        return slice(b * P, b * P + rows(b))

    ctx = ExitStack()
    with ctx:
        def sb(name, shape, dt=F32):
            return ctx.enter_context(nc.sbuf_tensor(name, shape, dt))

        def sem(name):
            return ctx.enter_context(nc.semaphore(name))

        x = sb("x", [P, NB, D])
        h_parts = sb("h_parts", [P, 2, NB, 2, D], F16)
        adj_rows = sb("adj_rows", [P, 3, N])
        adj_scaled = sb("adj_scaled", [P, 2, N])
        adj16 = sb("adj16", [P, 2, N], F16)
        adjT = sb("adjT", [P, NB, N], F16)
        p_hi = sb("p_hi", [P, 2, N], F16)
        p_lo = sb("p_lo", [P, 2, N], F16)
        pT = sb("pT", [P, 2, 2 * NB * P], F16)
        work = sb("work", [P, 4, N])
        logits = work[:, 0:2, :]
        p_f32 = work[:, 2:4, :]
        yT_all = work[:, 0:2, :]
        raw = work[:, :, :].rearrange("p a n -> p (a n)")
        kh_raw = raw[:, 0:DT * NODE_HEADS * D].rearrange("p (h e f) -> p h e f", h=NODE_HEADS, e=DT)
        off = DT * NODE_HEADS * D
        square = {}
        for name in ("w_node", "wq", "wk", "wv", "w3"):
            square[name] = raw[:, off:off + DT * D].rearrange("p (e f) -> p e f", e=DT)
            off += DT * D
        k_sum = raw[:, off:off + DT * D].rearrange("p (e f) -> p e f", e=DT)
        assert off + DT * D <= 4 * N
        hT32 = sb("hT32", [P, DT, N])
        hT = sb("hT", [P, 2, DT, N], F16)
        t32 = sb("t32", [P, DT, BANK])
        tT = sb("tT", [P, 2, DT, N], F16)
        centred = sb("centred", [P, RING, D])
        y_rows = sb("y_rows", [P, 2, D])
        yT = sb("yT", [P, 2, DT, P])
        head_out = sb("head_out", [P, 2, D])
        wn_T = sb("wn_T", [P, DT, D])
        w_fin = sb("w_fin", [P, 4, DT, D])
        m_qk = sb("m_qk", [P, DT, D])
        mb_qk = sb("mb_qk", [P, DT])
        bnode = sb("bnode", [P, DT])
        bq_col = sb("bq_col", [P, DT])
        bnode_wide = sb("bnode_wide", [P, DT, P])
        bias0 = sb("bias0", [P, D])
        bv_all = sb("bv_all", [P, D])
        b3_all = sb("b3_all", [P, D])
        ts = sb("ts", [P, 1])
        one_minus_t = sb("one_minus_t", [P, 1])
        ident16 = sb("ident16", [P, P], F16)
        ident32 = sb("ident32", [P, P])
        ones = sb("ones", [P, P])
        minus_half = sb("minus_half", [P, NB])
        stats = sb("stats", [P, 4 * NB, 6])
        mean_var = sb("mean_var", [P, 4 * NB, 2])
        minus_mean = sb("minus_mean", [P, NB])
        var_eps = sb("var_eps", [P, 4 * NB])
        rstd = sb("rstd", [P, 4 * NB])
        rstd3 = sb("rstd3", [P, NB])
        row_max = sb("row_max", [P, 2 * NB])
        shift = sb("shift", [P, 2 * NB])
        den = sb("den", [P, 2 * NB])
        rden = sb("rden", [P, 2 * NB])
        deg = sb("deg", [P, NB])
        deg_eps = sb("deg_eps", [P, NB])
        dis = sb("dis", [P, NB])

        ps = ctx.enter_context(nc.psum_tensor("ps", [P, 8, BANK], F32))
        ps_flat = ps[:, :, :].rearrange("p a b -> p (a b)")
        ps16 = ps_flat.bitcast(F16)
        TRIPLES = (0, 3 * BANK)
        ps_turned = [ps16[:, 2 * at:2 * at + 2 * NB * P].rearrange("p (j i) -> p j i", i=P) for at in TRIPLES]
        ps_y = ps[:, 6, 0:D]
        ps_scores = [ps_flat[:, at:at + N] for at in TRIPLES]
        ps_yT = ps[:, 7, 0:DT * P].rearrange("p (d r) -> p d r", d=DT)
        ps_big = ps_flat[:, 0:6 * BANK].rearrange("p (d n) -> p d n", d=DT)

        x_loaded = [sem(f"x_loaded{i}") for i in range(3)]
        w_loaded = {n: sem(f"loaded_{n}") for n in ("k", "w_node", "wq", "wk", "wv", "w3", "w2",
                                                    "bnode", "bq", "bv", "b3", "t")}
        adj_loaded = [sem(f"adj_loaded{i}") for i in range(3)]
        ident_ready = sem("ident_ready")
        const_ready = sem("const_ready")
        ksum_ready = sem("ksum_ready")
        bwide_ready = sem("bwide_ready")
        wt_mm = sem("wt_mm")
        wt_ready = sem("wt_ready")
        wprod_mm = sem("wprod_mm")
        wprod_ready = sem("wprod_ready")
        w2_ready = sem("w2_ready")
        omt_ready = sem("omt_ready")
        ps_cleared = sem("ps_cleared")
        stats_ready = sem("stats_ready")
        mv_ready = sem("mv_ready")
        ve0_ready = sem("ve0_ready")
        rstd0_ready = sem("rstd0_ready")
        ve_ready = sem("ve_ready")
        rstd3_ready = sem("rstd3_ready")
        rstd_ready = sem("rstd_ready")
        mmean_ready = sem("mmean_ready")
        centred0_act = sem("centred0_act")
        centred_ready = sem("centred_ready")
        hi0_pool = sem("hi0_pool")
        hi_ready = sem("hi_ready")
        lo_ready = sem("lo_ready")
        x_added = sem("x_added")
        xb_ready = sem("xb_ready")
        max_ready = sem("max_ready")
        shift_ready = sem("shift_ready")
        exp_ready = sem("exp_ready")
        exp32_ready = sem("exp32_ready")
        plo_ready = sem("plo_ready")
        adj_scaled_ready = sem("adj_scaled_ready")
        deg_ready = sem("deg_ready")
        dege_ready = sem("dege_ready")
        dis_ready = sem("dis_ready")
        rden_ready = sem("rden_ready")
        p_turned = sem("p_turned")
        pT_ready = sem("pT_ready")
        adj_turned = sem("adj_turned")
        adjT_ready = sem("adjT_ready")
        y_mm = sem("y_mm")
        y_ready = sem("y_ready")
        y_turned = sem("y_turned")
        yT_ready = sem("yT_ready")
        fin_mm = sem("fin_mm")
        head_ready = sem("head_ready")
        hT_mm = sem("hT_mm")
        hT32_ready = sem("hT32_ready")
        hThi_ready = sem("hThi_ready")
        hTlo_ready = sem("hTlo_ready")
        t_mm = sem("t_mm")
        t32_ready = sem("t32_ready")
        tThi_ready = sem("tThi_ready")
        tTlo_ready = sem("tTlo_ready")
        scores_mm = sem("scores_mm")
        logits_ready = max_ready
        big_mm = sem("big_mm")
        big_out = sem("big_out")
        big_out_act = sem("big_out_act")
        stored = sem("stored")

        block = ctx.enter_context(nc.Block())

        def adj_landed(eng, m):
            eng.wait_ge(adj_loaded[m % 3], 16 * (m // 3 + 1))

        def load_of(b):
            return [k for k, (a, z) in enumerate(LOADS) if a <= b < z][0]

        def wait_centred(eng, n):
            if n < NB and n % 2 == 0:
                eng.wait_ge(centred0_act, n // 2 + 1)
            else:
                eng.wait_ge(centred_ready, n // 2 + 1 if n < NB else NB // 2 + n - NB + 1)

        def wait_hi(eng, n):
            if n < NB and n % 2:
                eng.wait_ge(hi0_pool, n // 2 + 1)
            else:
                eng.wait_ge(hi_ready, n // 2 + 1 if n < NB else NB // 2 + n - NB + 2)

        def dram_rows(t, b):
            return t[b * P:b * P + rows(b), :]

        @block.sync
        def _(sp):
            def tiles(t):
                return t.rearrange("(e p) f -> p e f", p=P)

            def column(v, e):
                return v[e * P:(e + 1) * P].rearrange("(p a) -> p a", a=1)

            def load_weights_early():
                sp.dma_start(square["w_node"], tiles(w_node)).then_inc(w_loaded["w_node"], 16)
                sp.dma_start(kh_raw.rearrange("p h e f -> p (h e) f"),
                             k_heads.rearrange("h (e p) f -> p (h e) f", p=P)).then_inc(w_loaded["k"], 16)
                for e in range(DT):
                    sp.dma_start(bnode[:, e:e + 1], column(b_node, e)).then_inc(w_loaded["bnode"], 16)

            def load_weights():
                for name, w in (("wv", wv), ("w3", w3), ("wq", wq), ("wk", wk)):
                    sp.dma_start(square[name], tiles(w)).then_inc(w_loaded[name], 16)
                for e in range(DT):
                    sp.dma_start(bq_col[:, e:e + 1], column(bq, e)).then_inc(w_loaded["bq"], 16)
                sp.dma_start(w_fin[:, 2], tiles(w2)).then_inc(w_loaded["w2"], 16)
                for name, to, v, n in (("t", ts, t_in, 1), ("bv", bv_all, bv, D), ("b3", b3_all, b3, D)):
                    sp.dma_start(to[:, :], v.rearrange("(a n) -> a n", a=1).to_broadcast([P, n])
                                 ).then_inc(w_loaded[name], 16)

            for i, (a, z) in enumerate(LOADS[:-1]):
                sp.dma_start(x[:, a:z, :], x_in[a * P:z * P, :].rearrange("(b p) d -> p b d", p=P)
                             ).then_inc(x_loaded[i], 16)
            sp.dma_start(x[0:LAST, NB - 1, :], dram_rows(x_in, NB - 1)).then_inc(x_loaded[2], 16)
            for m in range(2 * NB):
                b = m % NB
                if m >= 3:
                    old = m - 3
                    if old < NB:
                        sp.wait_ge(exp_ready, old + 1)
                    else:
                        sp.wait_ge(adj_scaled_ready, old - NB + 1)
                        sp.wait_ge(deg_ready, old - NB + 1)
                sp.dma_start(adj_rows[0:rows(b), m % 3, :], dram_rows(adj, b)).then_inc(adj_loaded[m % 3], 16)
                if m == 1:
                    load_weights_early()
                if m == 2:
                    load_weights()
            for b in range(NB):
                sp.wait_ge(x_added, 3 * NB + b + 1)
                sp.dma_start(dram_rows(out, b), x[0:rows(b), b, :]).then_inc(stored, 16)
            sp.wait_ge(stored, 16 * NB)

        @block.gpsimd
        def _(pool):
            g = nc.gpsimd
            g.memset(ident16[:, :], 0.0).then_inc(ident_ready, 1)
            g.memset(ident32[:, :], 0.0).then_inc(ident_ready, 1)
            g.memset(minus_half[:, :], -0.5).then_inc(const_ready, 1)
            g.memset(ones[:, :], 1.0).then_inc(const_ready, 1)
            pool.wait_ge(ident_ready, 2)
            for m in (ident16, ident32):
                g.affine_select(out=m[:, :], in_=m[:, :], compare_op=ALU.not_equal, fill=1.0, base=0,
                                pattern=[[-1, P]], channel_multiplier=1).then_inc(ident_ready, 1)
            pool.wait_ge(const_ready, 2)

            def ln_scale(n):
                layer, b = divmod(n, NB)
                r = rows(b)
                pool.wait_ge(mv_ready, n + 1)
                g.tensor_scalar(var_eps[0:r, n:n + 1], mean_var[0:r, n, 1:2], H_SCALE ** -2, LN_EPS * H_SCALE ** -2,
                                ALU.mult, ALU.add).then_inc(ve_ready, 1)
                pool.wait_ge(ve_ready, n - NB + 1)
                if layer < 3:
                    g.tensor_tensor(rstd[0:r, n:n + 1], var_eps[0:r, n:n + 1], minus_half[0:r, 0:1],
                                    ALU.pow).then_inc(rstd_ready, 1)
                    return
                g.tensor_tensor(rstd3[0:r, b:b + 1], var_eps[0:r, n:n + 1], minus_half[0:r, 0:1],
                                ALU.pow).then_inc(rstd3_ready, 1)
                pool.wait_ge(rstd3_ready, b + 1)
                pool.wait_ge(dis_ready, b + 1)
                g.tensor_tensor(rstd[0:r, n:n + 1], rstd3[0:r, b:b + 1], dis[0:r, b:b + 1],
                                ALU.mult).then_inc(rstd_ready, 1)

            def split_hT(b):
                pool.wait_ge(hT32_ready, b + 1)
                g.tensor_scalar(hT[:, 0, :, cols(b)], hT32[:, :, cols(b)], 1.0, 1.0,
                                ALU.mult, ALU.mult).then_inc(hThi_ready, 1)
                pool.wait_ge(hThi_ready, b + 1)
                g.tensor_tensor(hT[:, 1, :, cols(b)], hT32[:, :, cols(b)], hT[:, 0, :, cols(b)],
                                ALU.subtract).then_inc(hTlo_ready, 1)

            def t_hi(c):
                a, w = CHUNKS[c]
                pool.wait_ge(t32_ready, 2 * c + 2)
                g.tensor_scalar(tT[:, 0, :, a:a + w], t32[:, :, 0:w], 1.0, 1.0,
                                ALU.mult, ALU.mult).then_inc(tThi_ready, 1)

            def prepare_weights():
                pool.wait_ge(w_loaded["k"], 16)
                g.tensor_tensor(k_sum, kh_raw[:, 0], kh_raw[:, 1], ALU.add).then_inc(ksum_ready, 1)
                g.tensor_tensor(kh_raw[:, 2], kh_raw[:, 2], kh_raw[:, 3], ALU.add).then_inc(ksum_ready, 1)
                pool.wait_ge(ksum_ready, 2)
                g.tensor_tensor(k_sum, k_sum, kh_raw[:, 2], ALU.add).then_inc(ksum_ready, 1)
                pool.wait_ge(ksum_ready, 3)
                g.tensor_scalar(k_sum, k_sum, 1.0 / NODE_HEADS, 1.0 / H_SCALE, ALU.mult, ALU.mult
                                ).then_inc(ksum_ready, 1)
                pool.wait_ge(w_loaded["bnode"], 16 * DT)
                for e in range(DT):
                    g.tensor_scalar(bnode_wide[:, e, :], ones[:, :], bnode[:, e:e + 1], H_SCALE,
                                    ALU.mult, ALU.mult).then_inc(bwide_ready, 1)
                pool.wait_ge(w_loaded["t"], 16)
                g.tensor_scalar(one_minus_t[:, :], ts[:, :], -1.0, 1.0, ALU.mult, ALU.add).then_inc(omt_ready, 1)

            for k, (a, z) in enumerate(LOADS):
                r = rows(a)
                pool.wait_ge(mv_ready, z)
                g.tensor_scalar(minus_mean[0:r, a:z], mean_var[0:r, a:z, 0], -1.0, 1.0, ALU.mult, ALU.mult
                                ).then_inc(mmean_ready, 1)
                g.tensor_scalar(var_eps[0:r, a:z], mean_var[0:r, a:z, 1], H_SCALE ** -2, LN_EPS * H_SCALE ** -2,
                                ALU.mult, ALU.add).then_inc(ve0_ready, 1)
                pool.wait_ge(ve0_ready, k + 1)
                g.tensor_tensor(rstd[0:r, a:z], var_eps[0:r, a:z], minus_half[0:r, 0:z - a], ALU.pow
                                ).then_inc(rstd0_ready, 1)
            for b in range(1, NB, 2):
                wait_centred(pool, b)
                g.tensor_scalar(h_parts[:, 0, b, 0, :], centred[:, b % RING, :], rstd[:, b:b + 1], 1.0,
                                ALU.mult, ALU.mult).then_inc(hi0_pool, 1)
            prepare_weights()
            for s in range(NB + L0_HT + 1):
                if 0 <= s - L0_FIN < NB:
                    ln_scale(NB + s - L0_FIN)
                if s == T_STEP:
                    t_hi(0)
                if 0 <= s - L0_HT and s < NB:
                    split_hT(s - L0_HT)

            def scale_adj(b):
                adj_landed(pool, NB + b)
                if b >= 2:
                    pool.wait_ge(logits_ready, NB + b - 1)
                g.tensor_scalar(adj_scaled[0:rows(b), b % 2, :], adj_rows[0:rows(b), (NB + b) % 3, :],
                                2.0, S_UNIT, ALU.mult, ALU.mult).then_inc(adj_scaled_ready, 1)

            def add_bias(layer, b, bias):
                r = rows(b)
                wait_centred(pool, layer * NB + b)
                g.tensor_tensor(x[0:r, b, :], x[0:r, b, :], bias[0:r, :], ALU.add).then_inc(xb_ready, 1)

            pool.wait_ge(w_loaded["bv"], 16)
            pool.wait_ge(x_added, NB)
            scale_adj(0)
            scale_adj(1)
            for s in range(NB + 4):
                if s < NCH - 1:
                    t_hi(s + 1)
                if 0 <= s - 4 < NB:
                    ln_scale(2 * NB + s - 4)
                if 2 <= s + 1 < NB:
                    scale_adj(s + 1)
                if s < NB:
                    add_bias(1, s, bv_all)
            for b in range(NB):
                r = rows(b)
                pool.wait_ge(deg_ready, b + 1)
                g.tensor_scalar(deg_eps[0:r, b:b + 1], deg[0:r, b:b + 1], 1.0, DEG_EPS, ALU.mult, ALU.add
                                ).then_inc(dege_ready, 1)
                pool.wait_ge(dege_ready, b + 1)
                g.tensor_tensor(dis[0:r, b:b + 1], deg_eps[0:r, b:b + 1], minus_half[0:r, 0:1], ALU.pow
                                ).then_inc(dis_ready, 1)
            pool.wait_ge(w_loaded["b3"], 16)
            for b in range(NB):
                ln_scale(3 * NB + b)
            for b in range(NB):
                add_bias(3, b, b3_all)

        @block.scalar
        def _(act):
            s_ = nc.scalar

            def ln_hi(n):
                layer, b = divmod(n, NB)
                r = rows(b)
                wait_centred(act, n)
                if layer:
                    act.wait_ge(rstd_ready, n - NB + 1)
                else:
                    act.wait_ge(rstd0_ready, load_of(b) + 1)
                if layer >= 2:
                    act.wait_ge(y_mm, NB * (layer - 1))
                s_.activation(h_parts[0:r, layer % 2, b, 0, :], centred[0:r, n % RING, :], ACT.Copy,
                              scale=rstd[0:r, n:n + 1]).then_inc(hi_ready, 1)

            def exp0(b):
                r = rows(b)
                act.wait_ge(shift_ready, b + 1)
                adj_landed(act, b)
                if b >= 2:
                    act.wait_ge(p_turned, b - 1)
                s_.activation(p_hi[0:r, b % 2, :], adj_rows[0:r, b % 3, :], ACT.Exp, bias=shift[0:r, b:b + 1],
                              scale=NEG, accum_out=den[0:r, b:b + 1]).then_inc(exp_ready, 1)

            def out_pT0(b):
                act.wait_ge(p_turned, b + 1)
                if b >= 2:
                    act.wait_ge(y_mm, b - 1)
                s_.activation(pT[:, b % 2, 0:NB * P].rearrange("p (j i) -> p j i", j=NB)[:, :, 0:rows(b)],
                              ps_turned[b % 2][:, 0:NB, 0:rows(b)], ACT.Copy).then_inc(pT_ready, 1)

            def degree(b):
                r = rows(b)
                adj_landed(act, NB + b)
                if b:
                    act.wait_ge(deg_ready, b)
                if b >= 2:
                    act.wait_ge(adj_turned, b - 1)
                s_.activation(adj16[0:r, b % 2, :], adj_rows[0:r, (NB + b) % 3, :], ACT.Copy,
                              accum_out=deg[0:r, b:b + 1]).then_inc(deg_ready, 1)

            def out_adjT(b):
                act.wait_ge(adj_turned, b + 1)
                src = ps_turned[(b + 1) % 2]
                s_.activation(adjT[:, 0:NB - 1, cols(b)], src[:, 0:NB - 1, 0:rows(b)], ACT.Copy)
                s_.activation(adjT[0:LAST, NB - 1, cols(b)], src[0:LAST, NB - 1, 0:rows(b)], ACT.Copy
                              ).then_inc(adjT_ready, 1)

            def out_y(n):
                r = rows(n % NB)
                act.wait_ge(y_mm, n + 1)
                act.wait_ge(rden_ready, n + 1)
                if n >= 2:
                    act.wait_ge(y_turned, n - 1)
                s_.activation(y_rows[0:r, n % 2, :], ps_y[0:r, :], ACT.Copy, scale=rden[0:r, n:n + 1]
                              ).then_inc(y_ready, 1)

            def out_yT(n):
                r = rows(n % NB)
                act.wait_ge(y_turned, n + 1)
                if n >= 2:
                    act.wait_ge(fin_mm, n - 1)
                s_.activation(yT[:, n % 2, :, 0:r], ps_yT[:, :, 0:r], ACT.Copy).then_inc(yT_ready, 1)

            def out_hT(b):
                act.wait_ge(hT_mm, b + 1)
                s_.activation(hT32[:, :, cols(b)], ps[:, 2, 0:DT * P].rearrange("p (d r) -> p d r", d=DT)[:, :, 0:rows(b)],
                              ACT.Copy).then_inc(hT32_ready, 1)

            def hT_hi(b):
                act.wait_ge(hT32_ready, b + 1)
                s_.activation(hT[:, 0, :, cols(b)], hT32[:, :, cols(b)], ACT.Copy).then_inc(hThi_ready, 1)

            def out_t(c):
                a, w = CHUNKS[c]
                for d in range(DT):
                    act.wait_ge(t_mm, DT * c + d + 1)
                    if c:
                        act.wait_ge(tTlo_ready, c)
                    s_.activation(t32[:, d, 0:w], ps[:, T_BANKS[c][d], 0:w], ACT.Identity, bias=mb_qk[:, d:d + 1],
                                  scale=T_SCALE / H_SCALE).then_inc(t32_ready, 1)

            def out_weight(to, bank, done, count, ready, scale=1.0):
                act.wait_ge(done, count)
                s_.activation(to, ps[:, bank, :].rearrange("p (e f) -> p e f", e=DT), ACT.Copy, scale=scale
                              ).then_inc(ready, 1)

            def out_weights(s):
                if s == 0:
                    out_weight(wn_T[:, :, :], 5, wt_mm, 1, wt_ready)
                if s == 1:
                    out_weight(w_fin[:, 0], 5, wprod_mm, 1, wprod_ready)
                    act.wait_ge(wprod_mm, 2)
                    s_.activation(bias0[:, :], ps[:, 7, 0:D], ACT.Copy).then_inc(wprod_ready, 1)
                    out_weight(w_fin[:, 1], 2, wt_mm, 2, wt_ready, 1.0 / H_SCALE)
                if s == 2:
                    out_weight(w_fin[:, 3], 2, wt_mm, 3, wt_ready, 1.0 / H_SCALE)
                if s == 3:
                    out_weight(m_qk[:, :, :], 2, wprod_mm, 3, wprod_ready)
                if s == 4:
                    act.wait_ge(wprod_mm, 4)
                    s_.activation(mb_qk[:, :], ps[:, 2, 0:DT], ACT.Copy, scale=T_SCALE).then_inc(wprod_ready, 1)
                    act.wait_ge(w_loaded["w2"], 16)
                    s_.activation(w_fin[:, 2], w_fin[:, 2], ACT.Copy, scale=1.0 / H_SCALE).then_inc(w2_ready, 1)

            def ln_centre_act(b):
                r = rows(b)
                act.wait_ge(mmean_ready, load_of(b) + 1)
                if b >= RING:
                    act.wait_ge(lo_ready, b - RING + 1)
                s_.activation(centred[0:r, b % RING, :], x[0:r, b, :], ACT.Relu, bias=minus_mean[0:r, b:b + 1]
                              ).then_inc(centred0_act, 1)

            for b in range(0, RING - 2, 2):
                ln_centre_act(b)
            for b in range(0, NB, 2):
                if b + RING - 2 < NB:
                    ln_centre_act(b + RING - 2)
                ln_hi(b)
                if b in (0, 2):
                    exp0(b // 2)
                if b == 6:
                    out_pT0(0)
            for s in range(NB + L0_HT + 1):
                if 0 < s < NB - 1:
                    exp0(s + 1)
                if 0 < s < NB:
                    out_pT0(s)
                if 0 <= s - L0_TURN_Y < NB:
                    out_yT(s - L0_TURN_Y)
                out_weights(s)
                if s == NB:
                    degree(0)
                if 0 <= s - 1 < NB:
                    out_y(s - 1)
                if 0 <= s - L0_FIN < NB:
                    ln_hi(NB + s - L0_FIN)
                if s == T_STEP:
                    out_t(0)
                if 0 <= s - L0_HT < NB:
                    out_hT(s - L0_HT)
                    if s >= NB:
                        hT_hi(s - L0_HT)
                if s == NB + 1:
                    out_adjT(0)

            def exp1(b):
                r = rows(b)
                n = NB + b
                act.wait_ge(shift_ready, n + 1)
                if b >= 2:
                    act.wait_ge(p_turned, n - 1)
                    act.wait_ge(plo_ready, b - 1)
                s_.activation(p_hi[0:r, b % 2, :], logits[0:r, b % 2, :], ACT.Exp, bias=shift[0:r, n:n + 1]
                              ).then_inc(exp_ready, 1)
                s_.activation(p_f32[0:r, b % 2, :], logits[0:r, b % 2, :], ACT.Exp, bias=shift[0:r, n:n + 1],
                              accum_out=den[0:r, n:n + 1]).then_inc(exp32_ready, 1)

            for s in range(NB + 4):
                if 0 <= s - 3 < NB:
                    out_y(NB + s - 3)
                if 1 <= s - 2 < NB:
                    out_adjT(s - 2)
                if 0 <= s - 4 < NB:
                    ln_hi(2 * NB + s - 4)
                if 1 < s < NB:
                    degree(s)
                if 0 <= s - 3 < NB:
                    out_yT(NB + s - 3)
                if s < NB:
                    exp1(s)
                if s == 1:
                    degree(s)
                if s < NCH - 1:
                    out_t(s + 1)
            act.wait_ge(omt_ready, 1)
            for b in range(NB):
                act.wait_ge(hT_mm, NB + b + 1)
                s_.activation(hT32[:, :, cols(b)],
                              ps[:, 6 + b % 2, 0:DT * P].rearrange("p (d r) -> p d r", d=DT)[:, :, 0:rows(b)],
                              ACT.Copy, scale=one_minus_t[:, 0:1]
                              ).then_inc(hT32_ready, 1)
            for b in range(NB):
                ln_hi(3 * NB + b)
            for c, (a, w) in enumerate(CHUNKS):
                act.wait_ge(big_mm, NCH + c + 1)
                s_.activation(yT_all[:, 1, a:a + w], ps_big[:, 1, a:a + w], ACT.Copy).then_inc(big_out_act, 1)

        @block.vector
        def _(dve):
            v = nc.vector

            def ln_stats(n):
                layer, b = divmod(n, NB)
                r = rows(b)
                if layer == 0:
                    dve.wait_ge(x_loaded[load_of(b)], 16)
                else:
                    dve.wait_ge(x_added, n - NB + 1)
                v.bn_stats(stats[0:r, n, :], x[0:r, b, :]).then_inc(stats_ready, 1)
                if layer:
                    ln_aggr(n)

            def ln_aggr(n):
                r = rows(n % NB)
                dve.wait_ge(stats_ready, n + 1)
                v.bn_aggr(mean_var[0:r, n, :], stats[0:r, n, :]).then_inc(mv_ready, 1)

            def ln_centre(n):
                layer, b = divmod(n, NB)
                r = rows(b)
                dve.wait_ge(mv_ready, n + 1)
                if n >= RING:
                    dve.wait_ge(lo_ready, n - RING + 1)
                v.tensor_scalar(centred[0:r, n % RING, :], x[0:r, b, :], mean_var[0:r, n, 0:1], 0.0,
                                ALU.subtract, ALU.max).then_inc(centred_ready, 1)

            def ln_lo(n):
                layer, b = divmod(n, NB)
                r = rows(b)
                wait_hi(dve, n)
                wait_centred(dve, n)
                if layer >= 2:
                    dve.wait_ge(y_mm, NB * (layer - 1))
                v.scalar_tensor_tensor(out=h_parts[0:r, layer % 2, b, 1, :], in0=centred[0:r, n % RING, :],
                                       scalar=rstd[0:r, n:n + 1], in1=h_parts[0:r, layer % 2, b, 0, :],
                                       op0=ALU.mult, op1=ALU.subtract).then_inc(lo_ready, 1)

            def max0(b):
                r = rows(b)
                adj_landed(dve, b)
                v.tensor_reduce(row_max[0:r, b:b + 1], adj_rows[0:r, b % 3, :], AX.X, ALU.max).then_inc(max_ready, 1)
                dve.wait_ge(max_ready, b + 1)
                v.tensor_scalar(shift[0:r, b:b + 1], row_max[0:r, b:b + 1], -NEG, None, ALU.mult
                                ).then_inc(shift_ready, 1)

            def out_pT(n):
                b = n % NB
                to = pT[:, n % 2, :].rearrange("p (k j i) -> p k j i", k=2, i=P)
                src = ps_turned[b % 2].rearrange("p (k j) i -> p k j i", k=2)
                dve.wait_ge(p_turned, n + 1)
                dve.wait_ge(y_mm, n - 1)
                v.tensor_copy(to[:, :, 0:NB - 1, 0:rows(b)], src[:, :, 0:NB - 1, 0:rows(b)])
                v.tensor_copy(to[0:LAST, :, NB - 1, 0:rows(b)], src[0:LAST, :, NB - 1, 0:rows(b)]).then_inc(pT_ready, 1)

            def inverse(n):
                r = rows(n % NB)
                if n < NB:
                    dve.wait_ge(exp_ready, n + 1)
                else:
                    dve.wait_ge(exp32_ready, n - NB + 1)
                v.reciprocal(rden[0:r, n:n + 1], den[0:r, n:n + 1]).then_inc(rden_ready, 1)

            def hT_lo(b):
                dve.wait_ge(hThi_ready, b + 1)
                v.tensor_tensor(hT[:, 1, :, cols(b)], hT32[:, :, cols(b)], hT[:, 0, :, cols(b)],
                                ALU.subtract).then_inc(hTlo_ready, 1)

            def t_lo(c):
                a, w = CHUNKS[c]
                dve.wait_ge(t32_ready, 2 * c + 2)
                dve.wait_ge(tThi_ready, c + 1)
                v.tensor_tensor(tT[:, 1, :, a:a + w], t32[:, :, 0:w], tT[:, 0, :, a:a + w],
                                ALU.subtract).then_inc(tTlo_ready, 1)

            def add0(b):
                r = rows(b)
                dve.wait_ge(fin_mm, b + 1)
                if b == 0:
                    dve.wait_ge(wprod_ready, 2)
                if b >= 2:
                    dve.wait_ge(x_added, b - 1)
                v.tensor_tensor(head_out[0:r, b % 2, :], ps[0:r, 5, 0:D], bias0[0:r, :], ALU.add
                                ).then_inc(head_ready, 1)
                dve.wait_ge(head_ready, b + 1)
                v.scalar_tensor_tensor(out=x[0:r, b, :], in0=head_out[0:r, b % 2, :], scalar=0.0, in1=x[0:r, b, :],
                                       op0=ALU.max, op1=ALU.add).then_inc(x_added, 1)

            for at in TRIPLES:
                v.memset(ps_flat[:, at + (NB - 1) * P // 2:at + NB * P // 2], 0.0).then_inc(ps_cleared, 1)
            for b in range(NB):
                ln_stats(b)
                if b:
                    ln_aggr(b - 1)
            ln_aggr(NB - 1)
            for b in range(1, RING - 1, 2):
                ln_centre(b)
            max0(0)
            max0(1)
            for b in range(NB):
                ln_lo(b)
                if b % 2 == 0 and b + RING - 1 < NB:
                    ln_centre(b + RING - 1)
            inverse(0)
            for s in range(NB + L0_HT + 1):
                if s < NB - 2:
                    max0(s + 2)
                if 0 <= s - L0_FIN - 1 and s <= NB:
                    ln_lo(NB + s - L0_FIN - 1)
                if 0 <= s - L0_FIN < NB:
                    add0(s - L0_FIN)
                    ln_stats(NB + s - L0_FIN)
                    ln_centre(NB + s - L0_FIN)
                if 0 < s < NB:
                    inverse(s)
                if NB <= s - 1 < NB + L0_HT:
                    hT_lo(s - 1 - L0_HT)
                if NB <= s < NB + L0_FIN:
                    ln_lo(NB + s - L0_FIN)
                if s == T_STEP:
                    t_lo(0)

            def logits_max(b):
                r = rows(b)
                n = NB + b
                dve.wait_ge(scores_mm, b + 1)
                dve.wait_ge(adj_scaled_ready, b + 1)
                if b >= 2:
                    dve.wait_ge(exp32_ready, b - 1)
                v.tensor_tensor_reduce(logits[0:r, b % 2, :], ps_scores[b % 2][0:r, :], adj_scaled[0:r, b % 2, :],
                                       1.0 / S_UNIT, -3.0e38, ALU.add, ALU.max, row_max[0:r, n:n + 1]
                                       ).then_inc(max_ready, 1)
                dve.wait_ge(max_ready, n + 1)
                v.tensor_scalar(shift[0:r, n:n + 1], row_max[0:r, n:n + 1], -1.0, LN2_15, ALU.mult, ALU.add
                                ).then_inc(shift_ready, 1)

            def p_low(b):
                r = rows(b)
                n = NB + b
                dve.wait_ge(exp_ready, n + 1)
                dve.wait_ge(exp32_ready, b + 1)
                if b >= 2:
                    dve.wait_ge(p_turned, n - 1)
                v.tensor_tensor(p_lo[0:r, b % 2, :], p_f32[0:r, b % 2, :], p_hi[0:r, b % 2, :], ALU.subtract
                                ).then_inc(plo_ready, 1)

            def add1(b):
                r = rows(b)
                dve.wait_ge(fin_mm, NB + b + 1)
                dve.wait_ge(xb_ready, b + 1)
                v.tensor_tensor(x[0:r, b, :], ps[0:r, 7, 0:D], x[0:r, b, :], ALU.add).then_inc(x_added, 1)

            for s in range(NB + 4):
                if 0 <= s - 4 < NB:
                    add1(s - 4)
                    ln_stats(2 * NB + s - 4)
                    ln_centre(2 * NB + s - 4)
                if s == 0:
                    logits_max(0)
                    logits_max(1)
                if 2 <= s < NB:
                    logits_max(s)
                if 0 <= s - 4 < NB:
                    ln_lo(2 * NB + s - 4)
                if 0 <= s - 1 < NB:
                    out_pT(NB + s - 1)
                if 0 <= s - 1 < NCH - 1:
                    t_lo(s)
                if s < NB:
                    p_low(s)
                    inverse(NB + s)

            dve.wait_ge(w_loaded["t"], 16)
            dve.wait_ge(hT32_ready, 2 * NB)
            def out_sums2(c):
                a, w = CHUNKS[c]
                dve.wait_ge(big_mm, c + 1)
                for d in range(DT):
                    v.scalar_tensor_tensor(out=yT_all[:, d, a:a + w], in0=ps_big[:, d, a:a + w], scalar=ts[:, 0:1],
                                           in1=hT32[:, d, a:a + w], op0=ALU.mult, op1=ALU.add).then_inc(big_out, 1)

            out_sums2(0)
            out_sums2(1)
            for b in range(NB + 2):
                if b < NB:
                    r = rows(b)
                    dve.wait_ge(fin_mm, 2 * NB + b + 1)
                    v.tensor_tensor(x[0:r, b, :], ps[0:r, 6 + b % 2, 0:D], x[0:r, b, :], ALU.add).then_inc(x_added, 1)
                if b == 0:
                    out_sums2(2)
                if 0 <= b - 1 < NB:
                    ln_stats(3 * NB + b - 1)
                    ln_centre(3 * NB + b - 1)
                if 0 <= b - 2:
                    ln_lo(3 * NB + b - 2)
            for c, (a, w) in enumerate(CHUNKS):
                dve.wait_ge(big_mm, NCH + c + 1)
                v.tensor_copy(yT_all[:, 0, a:a + w], ps_big[:, 0, a:a + w]).then_inc(big_out, 1)
            for b in range(NB):
                r = rows(b)
                dve.wait_ge(fin_mm, 3 * NB + b + 1)
                dve.wait_ge(xb_ready, NB + b + 1)
                v.scalar_tensor_tensor(out=x[0:r, b, :], in0=ps[0:r, 6 + b % 2, 0:D], scalar=dis[0:r, b:b + 1],
                                       in1=x[0:r, b, :], op0=ALU.mult, op1=ALU.add).then_inc(x_added, 1)

        @block.tensor
        def _(pe):
            t = nc.tensor
            def turn_weight(name, bank):
                pe.wait_ge(w_loaded[name], 16)
                for e in range(DT):
                    for d in range(DT):
                        last = t.transpose(ps[:, bank, e * D + d * P:e * D + (d + 1) * P],
                                           square[name][:, d, e * P:(e + 1) * P], ident32[:, :])
                last.then_inc(wt_mm, 1)

            def product(out_of, lhs, rhs):
                for m, o in enumerate(out_of):
                    for e in range(DT):
                        last = t.matmul(o, lhs(e, m), rhs(e), start=(e == 0), stop=(e == DT - 1))
                last.then_inc(wprod_mm, 1)

            def tile_of(w):
                return lambda e, m: w[:, e, m * P:(m + 1) * P]

            def prepare_weights(s):
                if s == 0:
                    turn_weight("w_node", 5)
                if s == 1:
                    pe.wait_ge(wt_ready, 1)
                    pe.wait_ge(ksum_ready, 4)
                    product([ps[:, 5, d * D:(d + 1) * D] for d in range(DT)], tile_of(wn_T), lambda e: k_sum[:, e, :])
                    pe.wait_ge(bwide_ready, DT)
                    product([ps[:, 7, 0:D]], lambda e, m: bnode_wide[:, e, :], lambda e: k_sum[:, e, :])
                    turn_weight("wv", 2)
                if s == 2:
                    pe.wait_ge(wt_ready, 2)
                    turn_weight("w3", 2)
                if s == 3:
                    pe.wait_ge(wt_ready, 3)
                    pe.wait_ge(w_loaded["wq"], 16)
                    pe.wait_ge(w_loaded["wk"], 16)
                    product([ps[:, 2, d * D:(d + 1) * D] for d in range(DT)], tile_of(square["wq"]),
                            lambda e: square["wk"][:, e, :])
                if s == 4:
                    pe.wait_ge(wprod_ready, 3)
                    pe.wait_ge(w_loaded["bq"], 16 * DT)
                    product([ps[:, 2, d:d + 1] for d in range(DT)], tile_of(square["wk"]),
                            lambda e: bq_col[:, e:e + 1])

            def turn(dst, src, b, at):
                r = rows(b)
                for j in range(NB):
                    last = t.transpose(dst[0:rows(j), at + j, 0:r], src[0:r, cols(j)],
                                       ident16[0:r, 0:r])
                return last

            def turn0(b):
                if b >= 2:
                    pe.wait_ge(pT_ready, b - 1)
                pe.wait_ge(exp_ready, b + 1)
                turn(ps_turned[b % 2], p_hi[:, b % 2, :], b, 0).then_inc(p_turned, 1)

            def turn_adj(b):
                if b == 0:
                    pe.wait_ge(pT_ready, NB - 1)
                elif b < NB - 1:
                    pe.wait_ge(logits_ready, NB + b + 2)
                else:
                    pe.wait_ge(pT_ready, 2 * NB - 1)
                pe.wait_ge(deg_ready, b + 1)
                turn(ps_turned[(b + 1) % 2], adj16[:, b % 2, :], b, 0).then_inc(adj_turned, 1)

            def weigh(n):
                layer, b = divmod(n, NB)
                r = rows(b)
                pe.wait_ge(pT_ready, n + 1)
                if n:
                    pe.wait_ge(y_ready, n)
                if n == NB:
                    pe.wait_ge(lo_ready, 2 * NB)
                    pe.wait_ge(t32_ready, DT * NCH)
                terms = [(0, 0), (0, 1)] + [(1, 0)] * layer
                for j in range(NB):
                    if n == 0:
                        pe.wait_ge(lo_ready, j + 1)
                    for k, (pp, hp) in enumerate(terms):
                        tile = pT[0:rows(j), n % 2, (pp * NB + j) * P:(pp * NB + j) * P + r]
                        last = t.matmul(ps_y[0:r, :], tile, h_parts[0:rows(j), layer % 2, j, hp, :],
                                        start=(j == 0 and k == 0), stop=(j == NB - 1 and k == len(terms) - 1))
                last.then_inc(y_mm, 1)

            def turn_y(n):
                r = rows(n % NB)
                pe.wait_ge(y_ready, n + 1)
                if n >= NB + 1:
                    pe.wait_ge(x_added, n)
                elif n:
                    pe.wait_ge(yT_ready, n)
                else:
                    pe.wait_ge(wprod_ready, 2)
                for d in range(DT):
                    last = t.transpose(ps_yT[:, d, 0:r], y_rows[0:r, n % 2, d * P:(d + 1) * P], ident32[0:r, 0:r])
                last.then_inc(y_turned, 1)

            def final(n, bank, left):
                layer, b = divmod(n, NB)
                r = rows(b)
                for d in range(DT):
                    last = t.matmul(ps[0:r, bank, 0:D], left(d), w_fin[:, layer, d, :],
                                    start=(d == 0), stop=(d == DT - 1))
                last.then_inc(fin_mm, 1)

            def final_att(n, bank):
                pe.wait_ge(yT_ready, n + 1)
                if bank == 5 and n:
                    pe.wait_ge(head_ready, n)
                    if n + L0_FIN > T_STEP:
                        pe.wait_ge(t32_ready, DT)
                final(n, bank, lambda d: yT[:, n % 2, d, 0:rows(n % NB)])

            def turn_h(n, bank):
                layer, b = divmod(n, NB)
                r = rows(b)
                pe.wait_ge(lo_ready, n + 1)
                for d in range(DT):
                    for part in range(2):
                        last = t.matmul(ps[:, bank, d * P:d * P + r],
                                        h_parts[0:r, layer % 2, b, part, d * P:(d + 1) * P],
                                        ident16[0:r, 0:r], start=(part == 0), stop=(part == 1))
                last.then_inc(hT_mm, 1)

            def make_t(c, halves=range(DT)):
                a, w = CHUNKS[c]
                last_block = min((c + 1) * BPC, NB)
                pe.wait_ge(hT32_ready, last_block)
                pe.wait_ge(head_ready, min(last_block + L0_HT - L0_FIN + 1, NB))
                if c:
                    pe.wait_ge(yT_ready, NB)
                for m in halves:
                    if c > 1:
                        pe.wait_ge(t32_ready, DT * (c - 1) + m + 1)
                    for d in range(DT):
                        last = t.matmul(ps[:, T_BANKS[c][m], 0:w], m_qk[:, d, m * P:(m + 1) * P], hT32[:, d, a:a + w],
                                        start=(d == 0), stop=(d == DT - 1))
                    last.then_inc(t_mm, 1)

            def scores(b, chunks):
                r = rows(b)
                pe.wait_ge(pT_ready, NB if b == 0 else NB + b - 1)
                if b == 0 and NCH - 1 in chunks:
                    pe.wait_ge(hT32_ready, NB)
                if b == 1:
                    pe.wait_ge(adjT_ready, 1)
                    if NCH - 1 in chunks:
                        pe.wait_ge(head_ready, NB)
                pe.wait_ge(tTlo_ready, b // BPC + 1)
                for c in chunks:
                    a, w = CHUNKS[c]
                    if b <= 1:
                        pe.wait_ge(hTlo_ready, min((c + 1) * BPC, NB))
                    terms = [(d, tp, hp) for d in range(DT) for tp, hp in ((0, 0), (0, 1), (1, 0))]
                    for k, (d, tp, hp) in enumerate(terms):
                        last = t.matmul(ps[0:r, 3 * (b % 2) + c, 0:w], tT[:, tp, d, cols(b)], hT[:, hp, d, a:a + w],
                                        start=(k == 0), stop=(k == len(terms) - 1))
                if NCH - 1 in chunks:
                    last.then_inc(scores_mm, 1)

            def gather(layer, j):
                par, r = layer % 2, rows(j)
                if layer == 2 and j == 0:
                    pe.wait_ge(logits_ready, 2 * NB)
                    pe.wait_ge(pT_ready, 2 * NB)
                    pe.wait_ge(adjT_ready, NB)
                pe.wait_ge(lo_ready, layer * NB + j + 1)
                if j < NB - 1:
                    for d in range(DT):
                        for part in range(2):
                            left = h_parts[0:r, par, j, part, d * P:(d + 1) * P]
                            for a, w in CHUNKS:
                                t.matmul(ps_big[:, d, a:a + w], left, adjT[0:r, j, a:a + w],
                                         start=(j == 0 and part == 0), stop=False)
                    return
                for a, w in CHUNKS:
                    for d in range(DT):
                        for part in range(2):
                            left = h_parts[0:r, par, j, part, d * P:(d + 1) * P]
                            last = t.matmul(ps_big[:, d, a:a + w], left, adjT[0:r, j, a:a + w],
                                            start=False, stop=(part == 1))
                    last.then_inc(big_mm, 1)

            pe.wait_ge(ident_ready, 4)
            pe.wait_ge(ps_cleared, 2)
            for s in range(NB + L0_HT + 1):
                if 0 <= s - L0_FIN < NB:
                    final_att(s - L0_FIN, 5)
                if s < NB:
                    turn0(s)
                if s == 0:
                    prepare_weights(0)
                if 0 <= s - L0_TURN_Y < NB:
                    turn_y(s - L0_TURN_Y)
                if 0 <= s - 1 < NB:
                    weigh(s - 1)
                if s:
                    prepare_weights(s)
                if s == T_STEP:
                    make_t(0)
                if s == NB + 1:
                    turn_adj(0)
                if s == NB + 2:
                    scores(0, [0])
                if s == NB + 3:
                    scores(0, [1])
                b = s - L0_HT
                if 0 <= b < NB:
                    if b == 0:
                        pe.wait_ge(wprod_ready, 4)
                    else:
                        pe.wait_ge(hT32_ready, b)
                        if s >= T_STEP:
                            pe.wait_ge(t32_ready, 1)
                    turn_h(NB + b, 2)
                if s == NB + 2:
                    scores(1, [0])
                if s == NB + 4:
                    scores(1, [1])


            def turn1(b):
                n = NB + b
                if b:
                    pe.wait_ge(adjT_ready, b)
                pe.wait_ge(exp_ready, n + 1)
                turn(ps_turned[b % 2], p_hi[:, b % 2, :], b, 0)
                pe.wait_ge(plo_ready, b + 1)
                turn(ps_turned[b % 2], p_lo[:, b % 2, :], b, NB).then_inc(p_turned, 1)

            for s in range(NB + 4):
                if 0 <= s - 4 < NB:
                    final_att(NB + s - 4, 7)
                if s == 0:
                    scores(0, [NCH - 1])
                    scores(1, [NCH - 1])
                    make_t(1)
                if 2 <= s < NB:
                    scores(s, range(NCH))
                if 0 <= s - 1 < NB:
                    turn1(s - 1)
                if s == 1:
                    make_t(2)
                if s <= NB:
                    if 0 <= s - 3:
                        turn_y(NB + s - 3)
                    if 0 <= s - 2:
                        weigh(NB + s - 2)
                if s == NB + 1:
                    weigh(NB + s - 2)
                    turn_y(NB + s - 3)
                    gather(2, 0)
                if s == NB + 2:
                    gather(2, 1)
                    turn_y(NB + s - 3)
                    gather(2, 2)
                if 1 <= s - 1 < NB:
                    turn_adj(s - 1)
            for j in range(NB):
                if j == 1:
                    pe.wait_ge(x_added, 2 * NB)
                if j >= 2:
                    pe.wait_ge(hT32_ready, NB + j - 1)
                turn_h(2 * NB + j, 6 + j % 2)
                if j % 2 and 3 + j // 2 < NB:
                    gather(2, 3 + j // 2)
            for j in range(3 + NB // 2, NB):
                gather(2, j)

            def final_big(layer, b):
                c = b // BPC
                if layer == 2:
                    pe.wait_ge(big_out, DT * (c + 1))
                    if b == 0:
                        pe.wait_ge(w2_ready, 1)
                else:
                    pe.wait_ge(big_out, DT * NCH + c + 1)
                    pe.wait_ge(big_out_act, c + 1)
                if b >= 2:
                    pe.wait_ge(x_added, layer * NB + b - 1)
                final(layer * NB + b, 6 + b % 2, lambda d: yT_all[:, d, cols(b)])

            nxt = 5
            for b in range(nxt):
                final_big(2, b)
            pe.wait_ge(big_out, DT * NCH)
            for j in range(NB):
                gather(3, j)
                for b in range(nxt, min(nxt + 2, NB)):
                    final_big(2, b)
                nxt += 2
            pe.wait_ge(x_added, 3 * NB)
            for b in range(NB):
                final_big(3, b)


INS = ["x", "adj", "L0_gnn_W_node", "L0_gnn_b_node", "L0_gnn_K", "L1_gnn_Wq", "L1_gnn_bq", "L1_gnn_Wk",
       "L1_gnn_Wv", "L1_gnn_bv", "L2_gnn_t", "L2_gnn_weight", "L3_gnn_W", "L3_gnn_b"]


def kernel(**inputs):
    import numpy as np
    import concourse.bacc as bacc
    from concourse.bass_utils import run_bass_kernel_spmd

    nc = bacc.Bacc("TRN2", target_bir_lowering=False, num_devices=1)
    arrays, args = {}, []
    for name in INS:
        a = np.ascontiguousarray(inputs[name])
        arrays[f"in_{name}"] = a
        args.append(nc.dram_tensor(f"in_{name}", a.shape, mybir.dt.from_np(a.dtype), kind="ExternalInput").ap())
    args.append(nc.dram_tensor("out_x", inputs["x"].shape, F32, kind="ExternalOutput").ap())
    build(nc, *args)
    r = run_bass_kernel_spmd(nc, [arrays], core_ids=[0])
    return r.results[0]["out_x"]
```

```python
from contextlib import ExitStack

import concourse.bass as bass
from concourse import mybir

F32 = mybir.dt.float32
F16 = mybir.dt.float16
ALU = mybir.AluOpType
ACT = mybir.ActivationFunctionType
AX = mybir.AxisListType

P = 128
BANK = 512
NEG = 1.0e10
LN_EPS = 1e-5
DEG_EPS = 1e-8
H_SCALE = 1024.0
T_SCALE = 0.5
W_SCALE = 256.0
LN2_15 = 10.397207708399179
NODE_HEADS = 4


def build(nc, x_in, adj, w_node, b_node, k_heads, wq, bq, wk, wv, bv, t_in, w2, w3, b3, out):
    N, D = x_in.shape
    NB = -(-N // P)
    LAST = N - (NB - 1) * P
    DT = D // P
    CHUNKS = [(c, min(BANK, N - c)) for c in range(0, N, BANK)]
    BPC = BANK // P
    NCH = len(CHUNKS)
    S_UNIT = H_SCALE * T_SCALE * float(D) ** 0.5
    EARLY = 3
    L0_TURN_Y, L0_FIN, L0_HT = 2, 3, 5
    T_STEP = BPC + L0_HT
    T_BANKS = [(5, 2)] + [(6, 7)] * (NCH - 1)
    LOADS = [(0, 5), (5, NB - 1), (NB - 1, NB)]
    RING = 4
    assert NCH == 3 and DT == 2 and LAST > 64

    def rows(b):
        return LAST if b == NB - 1 else P

    def cols(b):
        return slice(b * P, b * P + rows(b))

    ctx = ExitStack()
    with ctx:
        def sb(name, shape, dt=F32):
            return ctx.enter_context(nc.sbuf_tensor(name, shape, dt))

        def sem(name):
            return ctx.enter_context(nc.semaphore(name))

        x = sb("x", [P, NB, D])
        h_parts = sb("h_parts", [P, 2, NB, 2, D], F16)
        adj_rows = sb("adj_rows", [P, 3, N])
        adj_scaled = sb("adj_scaled", [P, 2, N])
        adj16 = sb("adj16", [P, 2, N], F16)
        adjT = sb("adjT", [P, NB, N], F16)
        p_hi = sb("p_hi", [P, 2, N], F16)
        p_lo = sb("p_lo", [P, 2, N], F16)
        pT = sb("pT", [P, 2, 2 * NB * P], F16)
        work = sb("work", [P, 4, N])
        logits = work[:, 0:2, :]
        p_f32 = work[:, 2:4, :]
        yT_all = work[:, 0:2, :]
        raw = work[:, :, :].rearrange("p a n -> p (a n)")
        kh_raw = raw[:, 0:DT * NODE_HEADS * D].rearrange("p (h e f) -> p h e f", h=NODE_HEADS, e=DT)
        off = DT * NODE_HEADS * D
        square = {}
        for name in ("w_node", "wq", "wk", "wv", "w3"):
            square[name] = raw[:, off:off + DT * D].rearrange("p (e f) -> p e f", e=DT)
            off += DT * D
        k_sum = raw[:, off:off + DT * D].rearrange("p (e f) -> p e f", e=DT)
        assert off + DT * D <= 4 * N
        centred0 = adjT[:, :, :].rearrange("p j i -> p (j i)").bitcast(F32)[:, 0:NB * D].rearrange(
            "p (b d) -> p b d", b=NB)
        hT32 = sb("hT32", [P, DT, N])
        hT = sb("hT", [P, 2, DT, N], F16)
        t32 = sb("t32", [P, DT, BANK])
        tT = sb("tT", [P, 2, DT, N], F16)
        centred = sb("centred", [P, RING, D])
        y_rows = sb("y_rows", [P, 2, D])
        yT = sb("yT", [P, 2, DT, P])
        y16 = y_rows[:, :, :].rearrange("p n f -> p (n f)").bitcast(F16).rearrange(
            "p (n k f) -> p n k f", n=2, k=2)
        yT16 = yT[:, :, :, :].rearrange("p n d r -> p (n d r)").bitcast(F16).rearrange(
            "p (n k r) -> p n k r", n=2, k=2 * DT)
        head_out = sb("head_out", [P, 2, D])
        wn_T = sb("wn_T", [P, DT, D])
        w_fin = sb("w_fin", [P, 4, DT, D])
        m32 = sb("m32", [P, DT, D])
        cut32 = (m32[:, :, :], w_fin[:, 1])
        cut = sb("cut", [P, 2, 2, DT, D], F16)
        m_qk, wv_T = cut[:, 0], cut[:, 1]
        mb_qk = sb("mb_qk", [P, DT])
        bnode = sb("bnode", [P, DT])
        bq_col = sb("bq_col", [P, DT])
        bnode_wide = sb("bnode_wide", [P, DT, P])
        bias0 = sb("bias0", [P, D])
        bv_all = sb("bv_all", [P, D])
        b3_all = sb("b3_all", [P, D])
        ts = sb("ts", [P, 1])
        one_minus_t = sb("one_minus_t", [P, 1])
        ident16 = sb("ident16", [P, P], F16)
        ident32 = sb("ident32", [P, P])
        ones = sb("ones", [P, P])
        minus_half = sb("minus_half", [P, NB])
        stats = sb("stats", [P, 4 * NB, 6])
        mean_var = sb("mean_var", [P, 4 * NB, 2])
        minus_mean = sb("minus_mean", [P, NB])
        var_eps = sb("var_eps", [P, 4 * NB])
        rstd = sb("rstd", [P, 4 * NB])
        rstd3 = sb("rstd3", [P, NB])
        row_max = sb("row_max", [P, 2 * NB])
        shift = sb("shift", [P, 2 * NB])
        den = sb("den", [P, 2 * NB])
        rden = sb("rden", [P, 2 * NB])
        deg = sb("deg", [P, NB])
        deg_eps = sb("deg_eps", [P, NB])
        dis = sb("dis", [P, NB])

        ps = ctx.enter_context(nc.psum_tensor("ps", [P, 8, BANK], F32))
        ps_flat = ps[:, :, :].rearrange("p a b -> p (a b)")
        ps16 = ps_flat.bitcast(F16)
        TRIPLES = (0, 3 * BANK)
        ps_turned = [ps16[:, 2 * at:2 * at + 2 * NB * P].rearrange("p (j i) -> p j i", i=P) for at in TRIPLES]
        ps_y = ps[:, 6, 0:D]
        ps_scores = [ps_flat[:, at:at + N] for at in TRIPLES]
        ps_yT = ps[:, 7, 0:DT * P].rearrange("p (d r) -> p d r", d=DT)
        ps_yT16 = ps16[:, 14 * BANK:14 * BANK + 2 * DT * P].rearrange("p (k r) -> p k r", k=2 * DT)
        ps_big = ps_flat[:, 0:6 * BANK].rearrange("p (d n) -> p d n", d=DT)

        x_loaded = [sem(f"x_loaded{i}") for i in range(len(LOADS))]
        w_loaded = {n: sem(f"loaded_{n}") for n in ("k", "w_node", "wq", "wk", "wv", "w3", "w2",
                                                    "bnode", "bq", "bv", "b3", "t")}
        adj_loaded = [sem(f"adj_loaded{i}") for i in range(3)]
        ident_ready = sem("ident_ready")
        const_ready = sem("const_ready")
        ksum_ready = sem("ksum_ready")
        bwide_ready = sem("bwide_ready")
        wt_mm = sem("wt_mm")
        wt_ready = sem("wt_ready")
        wprod_mm = sem("wprod_mm")
        wprod_ready = sem("wprod_ready")
        w2_ready = sem("w2_ready")
        cut_hi_ready = sem("cut_hi_ready")
        cut_lo_ready = sem("cut_lo_ready")
        omt_ready = sem("omt_ready")
        ps_cleared = sem("ps_cleared")
        stats_ready = sem("stats_ready")
        mv_ready = sem("mv_ready")
        ve0_ready = sem("ve0_ready")
        rstd0_ready = sem("rstd0_ready")
        ve_ready = sem("ve_ready")
        rstd3_ready = sem("rstd3_ready")
        rstd_ready = sem("rstd_ready")
        mmean_ready = sem("mmean_ready")
        centred0_act = sem("centred0_act")
        centred_ready = sem("centred_ready")
        hi0_pool = sem("hi0_pool")
        hi_ready = sem("hi_ready")
        lo_ready = sem("lo_ready")
        x_added = sem("x_added")
        xb_ready = sem("xb_ready")
        max_ready = sem("max_ready")
        shift_ready = sem("shift_ready")
        exp_ready = sem("exp_ready")
        exp32_ready = sem("exp32_ready")
        plo_ready = sem("plo_ready")
        adj_scaled_ready = sem("adj_scaled_ready")
        deg_ready = sem("deg_ready")
        dege_ready = sem("dege_ready")
        dis_ready = sem("dis_ready")
        rden_ready = sem("rden_ready")
        p_turned = sem("p_turned")
        pT_ready = sem("pT_ready")
        adj_turned = sem("adj_turned")
        adjT_ready = sem("adjT_ready")
        y_mm = sem("y_mm")
        y_ready = sem("y_ready")
        ylo_ready = sem("ylo_ready")
        y_turned = sem("y_turned")
        yT_ready = sem("yT_ready")
        fin_mm = sem("fin_mm")
        head_ready = sem("head_ready")
        hT_mm = sem("hT_mm")
        hT32_ready = sem("hT32_ready")
        hThi_ready = sem("hThi_ready")
        hTlo_ready = sem("hTlo_ready")
        t_mm = sem("t_mm")
        t32_ready = sem("t32_ready")
        tThi_ready = sem("tThi_ready")
        tTlo_ready = sem("tTlo_ready")
        scores_mm = sem("scores_mm")
        logits_ready = max_ready
        big_mm = sem("big_mm")
        big_out = sem("big_out")
        big_out_act = sem("big_out_act")
        scaled_ready = sem("scaled_ready")
        big_out_pool = sem("big_out_pool")
        stored = sem("stored")

        block = ctx.enter_context(nc.Block())

        def adj_landed(eng, m):
            eng.wait_ge(adj_loaded[m % 3], 16 * (m // 3 + 1))

        def load_of(b):
            return [k for k, (a, z) in enumerate(LOADS) if a <= b < z][0]

        def centred_of(n):
            return centred0[:, n, :] if n < NB else centred[:, n % RING, :]

        def wait_centred(eng, n):
            if n < NB and n % 2 == 0:
                eng.wait_ge(centred0_act, n // 2 + 1)
            else:
                eng.wait_ge(centred_ready, n // 2 + 1 if n < NB else NB // 2 + n - NB + 1)

        def wait_hi(eng, n):
            if n < NB and n % 2:
                eng.wait_ge(hi0_pool, n // 2 + 1)
            else:
                eng.wait_ge(hi_ready, n // 2 + 1 if n < NB else NB // 2 + n - NB + 2)

        def dram_rows(t, b):
            return t[b * P:b * P + rows(b), :]

        @block.sync
        def _(sp):
            def tiles(t):
                return t.rearrange("(e p) f -> p e f", p=P)

            def column(v, e):
                return v[e * P:(e + 1) * P].rearrange("(p a) -> p a", a=1)

            def load_weights_early():
                for name, w in (("w_node", w_node), ("wv", wv), ("w3", w3)):
                    sp.dma_start(square[name], tiles(w)).then_inc(w_loaded[name], 16)
                sp.dma_start(kh_raw.rearrange("p h e f -> p (h e) f"),
                             k_heads.rearrange("h (e p) f -> p (h e) f", p=P)).then_inc(w_loaded["k"], 16)
                for e in range(DT):
                    sp.dma_start(bnode[:, e:e + 1], column(b_node, e)).then_inc(w_loaded["bnode"], 16)

            def load_weights():
                for name, w in (("wq", wq), ("wk", wk)):
                    sp.dma_start(square[name], tiles(w)).then_inc(w_loaded[name], 16)
                for e in range(DT):
                    sp.dma_start(bq_col[:, e:e + 1], column(bq, e)).then_inc(w_loaded["bq"], 16)
                sp.dma_start(w_fin[:, 2], tiles(w2)).then_inc(w_loaded["w2"], 16)
                for name, to, v, n in (("t", ts, t_in, 1), ("bv", bv_all, bv, D), ("b3", b3_all, b3, D)):
                    sp.dma_start(to[:, :], v.rearrange("(a n) -> a n", a=1).to_broadcast([P, n])
                                 ).then_inc(w_loaded[name], 16)

            for i, (a, z) in enumerate(LOADS[:-1]):
                sp.dma_start(x[:, a:z, :], x_in[a * P:z * P, :].rearrange("(b p) d -> p b d", p=P)
                             ).then_inc(x_loaded[i], 16)
            sp.dma_start(x[0:LAST, NB - 1, :], dram_rows(x_in, NB - 1)).then_inc(x_loaded[2], 16)
            for m in range(2 * NB):
                b = m % NB
                if m >= 3:
                    old = m - 3
                    if old < NB:
                        sp.wait_ge(exp_ready, old + 1)
                    else:
                        sp.wait_ge(adj_scaled_ready, old - NB + 1)
                        sp.wait_ge(deg_ready, old - NB + 1)
                sp.dma_start(adj_rows[0:rows(b), m % 3, :], dram_rows(adj, b)).then_inc(adj_loaded[m % 3], 16)
                if m == 1:
                    load_weights_early()
                if m == 2:
                    load_weights()
            for b in range(NB):
                sp.wait_ge(x_added, 3 * NB + b + 1)
                sp.dma_start(dram_rows(out, b), x[0:rows(b), b, :]).then_inc(stored, 16)
            sp.wait_ge(stored, 16 * NB)

        @block.gpsimd
        def _(pool):
            g = nc.gpsimd
            g.memset(ident16[:, :], 0.0).then_inc(ident_ready, 1)
            g.memset(ident32[:, :], 0.0).then_inc(ident_ready, 1)
            g.memset(minus_half[:, :], -0.5).then_inc(const_ready, 1)
            g.memset(ones[:, :], 1.0).then_inc(const_ready, 1)
            pool.wait_ge(ident_ready, 2)
            for m in (ident16, ident32):
                g.affine_select(out=m[:, :], in_=m[:, :], compare_op=ALU.not_equal, fill=1.0, base=0,
                                pattern=[[-1, P]], channel_multiplier=1).then_inc(ident_ready, 1)
            pool.wait_ge(const_ready, 2)

            def ln_scale(n):
                layer, b = divmod(n, NB)
                r = rows(b)
                pool.wait_ge(mv_ready, n + 1)
                g.tensor_scalar(var_eps[0:r, n:n + 1], mean_var[0:r, n, 1:2], H_SCALE ** -2, LN_EPS * H_SCALE ** -2,
                                ALU.mult, ALU.add).then_inc(ve_ready, 1)
                pool.wait_ge(ve_ready, n - NB + 1)
                if layer < 3:
                    g.tensor_tensor(rstd[0:r, n:n + 1], var_eps[0:r, n:n + 1], minus_half[0:r, 0:1],
                                    ALU.pow).then_inc(rstd_ready, 1)
                    return
                g.tensor_tensor(rstd3[0:r, b:b + 1], var_eps[0:r, n:n + 1], minus_half[0:r, 0:1],
                                ALU.pow).then_inc(rstd3_ready, 1)
                pool.wait_ge(rstd3_ready, b + 1)
                pool.wait_ge(dis_ready, b + 1)
                g.tensor_tensor(rstd[0:r, n:n + 1], rstd3[0:r, b:b + 1], dis[0:r, b:b + 1],
                                ALU.mult).then_inc(rstd_ready, 1)

            def split_hT(b):
                pool.wait_ge(hT32_ready, b + 1)
                g.tensor_scalar(hT[:, 0, :, cols(b)], hT32[:, :, cols(b)], 1.0, 1.0,
                                ALU.mult, ALU.mult).then_inc(hThi_ready, 1)
                pool.wait_ge(hThi_ready, b + 1)
                g.tensor_tensor(hT[:, 1, :, cols(b)], hT32[:, :, cols(b)], hT[:, 0, :, cols(b)],
                                ALU.subtract).then_inc(hTlo_ready, 1)

            def t_hi(c):
                a, w = CHUNKS[c]
                pool.wait_ge(t32_ready, 2 * c + 2)
                g.tensor_scalar(tT[:, 0, :, a:a + w], t32[:, :, 0:w], 1.0, 1.0,
                                ALU.mult, ALU.mult).then_inc(tThi_ready, 1)

            def prepare_weights():
                pool.wait_ge(w_loaded["k"], 16)
                g.tensor_tensor(k_sum, kh_raw[:, 0], kh_raw[:, 1], ALU.add).then_inc(ksum_ready, 1)
                g.tensor_tensor(kh_raw[:, 2], kh_raw[:, 2], kh_raw[:, 3], ALU.add).then_inc(ksum_ready, 1)
                pool.wait_ge(ksum_ready, 2)
                g.tensor_tensor(k_sum, k_sum, kh_raw[:, 2], ALU.add).then_inc(ksum_ready, 1)
                pool.wait_ge(ksum_ready, 3)
                g.tensor_scalar(k_sum, k_sum, 1.0 / NODE_HEADS, 1.0 / H_SCALE, ALU.mult, ALU.mult
                                ).then_inc(ksum_ready, 1)
                pool.wait_ge(w_loaded["bnode"], 16 * DT)
                for e in range(DT):
                    g.tensor_scalar(bnode_wide[:, e, :], ones[:, :], bnode[:, e:e + 1], H_SCALE,
                                    ALU.mult, ALU.mult).then_inc(bwide_ready, 1)
                for k, (which, ready, count) in enumerate(((1, wt_ready, 2), (0, wprod_ready, 1))):
                    pool.wait_ge(ready, count)
                    g.tensor_scalar(cut[:, which, 0], cut32[which], 1.0, 1.0, ALU.mult, ALU.mult
                                    ).then_inc(cut_hi_ready, 1)
                    pool.wait_ge(cut_hi_ready, k + 1)
                    g.tensor_tensor(cut[:, which, 1], cut32[which], cut[:, which, 0], ALU.subtract
                                    ).then_inc(cut_lo_ready, 1)
                pool.wait_ge(w_loaded["t"], 16)
                g.tensor_scalar(one_minus_t[:, :], ts[:, :], -1.0, 1.0, ALU.mult, ALU.add).then_inc(omt_ready, 1)

            for k, (a, z) in enumerate(LOADS):
                r = rows(a)
                pool.wait_ge(mv_ready, z)
                g.tensor_scalar(minus_mean[0:r, a:z], mean_var[0:r, a:z, 0], -1.0, 1.0, ALU.mult, ALU.mult
                                ).then_inc(mmean_ready, 1)
                g.tensor_scalar(var_eps[0:r, a:z], mean_var[0:r, a:z, 1], H_SCALE ** -2, LN_EPS * H_SCALE ** -2,
                                ALU.mult, ALU.add).then_inc(ve0_ready, 1)
                pool.wait_ge(ve0_ready, k + 1)
                g.tensor_tensor(rstd[0:r, a:z], var_eps[0:r, a:z], minus_half[0:r, 0:z - a], ALU.pow
                                ).then_inc(rstd0_ready, 1)
            for b in range(1, NB, 2):
                wait_centred(pool, b)
                g.tensor_scalar(h_parts[:, 0, b, 0, :], centred_of(b), rstd[:, b:b + 1], 1.0,
                                ALU.mult, ALU.mult).then_inc(hi0_pool, 1)
            prepare_weights()
            for s in range(NB + L0_HT + 1):
                if 0 <= s - L0_FIN < NB:
                    ln_scale(NB + s - L0_FIN)
                if s == T_STEP:
                    t_hi(0)
                if 0 <= s - L0_HT and s < NB:
                    split_hT(s - L0_HT)

            def scale_adj(b):
                adj_landed(pool, NB + b)
                if b >= 2:
                    pool.wait_ge(logits_ready, NB + b - 1)
                g.tensor_scalar(adj_scaled[0:rows(b), b % 2, :], adj_rows[0:rows(b), (NB + b) % 3, :],
                                2.0, S_UNIT, ALU.mult, ALU.mult).then_inc(adj_scaled_ready, 1)

            def add_bias(layer, b, bias):
                r = rows(b)
                wait_centred(pool, layer * NB + b)
                g.tensor_tensor(x[0:r, b, :], x[0:r, b, :], bias[0:r, :], ALU.add).then_inc(xb_ready, 1)

            pool.wait_ge(w_loaded["bv"], 16)
            pool.wait_ge(x_added, NB)
            scale_adj(0)
            scale_adj(1)
            for s in range(NB + 4):
                if s < NCH - 1:
                    t_hi(s + 1)
                if 0 <= s - 4 < NB:
                    ln_scale(2 * NB + s - 4)
                if 2 <= s + 1 < NB:
                    scale_adj(s + 1)
                if s < NB:
                    add_bias(1, s, bv_all)
            for b in range(NB):
                r = rows(b)
                pool.wait_ge(deg_ready, b + 1)
                g.tensor_scalar(deg_eps[0:r, b:b + 1], deg[0:r, b:b + 1], 1.0, DEG_EPS, ALU.mult, ALU.add
                                ).then_inc(dege_ready, 1)
                pool.wait_ge(dege_ready, b + 1)
                g.tensor_tensor(dis[0:r, b:b + 1], deg_eps[0:r, b:b + 1], minus_half[0:r, 0:1], ALU.pow
                                ).then_inc(dis_ready, 1)
            pool.wait_ge(hT32_ready, 2 * NB)
            for c, (a, w) in enumerate(CHUNKS[1:]):
                pool.wait_ge(scaled_ready, c + 1)
                g.tensor_tensor(yT_all[:, 1, a:a + w], yT_all[:, 1, a:a + w], hT32[:, 1, a:a + w], ALU.add
                                ).then_inc(big_out_pool, 1)
            pool.wait_ge(w_loaded["b3"], 16)
            for b in range(NB):
                ln_scale(3 * NB + b)
            for b in range(NB):
                add_bias(3, b, b3_all)

        @block.scalar
        def _(act):
            s_ = nc.scalar

            def ln_hi(n):
                layer, b = divmod(n, NB)
                r = rows(b)
                wait_centred(act, n)
                if layer:
                    act.wait_ge(rstd_ready, n - NB + 1)
                else:
                    act.wait_ge(rstd0_ready, load_of(b) + 1)
                if layer >= 2:
                    act.wait_ge(y_mm, NB * (layer - 1))
                s_.activation(h_parts[0:r, layer % 2, b, 0, :], centred_of(n)[0:r, :], ACT.Copy,
                              scale=rstd[0:r, n:n + 1]).then_inc(hi_ready, 1)

            def exp0(b):
                r = rows(b)
                act.wait_ge(shift_ready, b + 1)
                adj_landed(act, b)
                if b >= 2:
                    act.wait_ge(p_turned, b - 1)
                s_.activation(p_hi[0:r, b % 2, :], adj_rows[0:r, b % 3, :], ACT.Exp, bias=shift[0:r, b:b + 1],
                              scale=NEG, accum_out=den[0:r, b:b + 1]).then_inc(exp_ready, 1)

            def out_pT0(b):
                act.wait_ge(p_turned, b + 1)
                if b >= 2:
                    act.wait_ge(y_mm, b - 1)
                s_.activation(pT[:, b % 2, 0:NB * P].rearrange("p (j i) -> p j i", j=NB)[:, :, 0:rows(b)],
                              ps_turned[b % 2][:, 0:NB, 0:rows(b)], ACT.Copy).then_inc(pT_ready, 1)

            def degree(b):
                r = rows(b)
                adj_landed(act, NB + b)
                if b:
                    act.wait_ge(deg_ready, b)
                if b >= 2:
                    act.wait_ge(adj_turned, b - 1)
                s_.activation(adj16[0:r, b % 2, :], adj_rows[0:r, (NB + b) % 3, :], ACT.Copy,
                              accum_out=deg[0:r, b:b + 1]).then_inc(deg_ready, 1)

            def out_adjT(b):
                act.wait_ge(adj_turned, b + 1)
                if b == 0:
                    act.wait_ge(lo_ready, NB)
                src = ps_turned[(b + 1) % 2]
                s_.activation(adjT[:, 0:NB - 1, cols(b)], src[:, 0:NB - 1, 0:rows(b)], ACT.Copy)
                s_.activation(adjT[0:LAST, NB - 1, cols(b)], src[0:LAST, NB - 1, 0:rows(b)], ACT.Copy
                              ).then_inc(adjT_ready, 1)

            def out_y(n):
                r = rows(n % NB)
                act.wait_ge(y_mm, n + 1)
                act.wait_ge(rden_ready, n + 1)
                if n >= 2:
                    act.wait_ge(y_turned, n - 1)
                to = y_rows[0:r, n % 2, :] if n < NB else y16[0:r, n % 2, 0, :]
                s_.activation(to, ps_y[0:r, :], ACT.Copy, scale=rden[0:r, n:n + 1]
                              ).then_inc(y_ready, 1)

            def out_yT(n):
                r = rows(n % NB)
                act.wait_ge(y_turned, n + 1)
                if n >= 2:
                    act.wait_ge(fin_mm, n - 1)
                if n < NB:
                    s_.activation(yT[:, n % 2, :, 0:r], ps_yT[:, :, 0:r], ACT.Copy).then_inc(yT_ready, 1)
                else:
                    s_.activation(yT16[:, n % 2, :, 0:r], ps_yT16[:, :, 0:r], ACT.Copy).then_inc(yT_ready, 1)

            def out_hT(b):
                act.wait_ge(hT_mm, b + 1)
                s_.activation(hT32[:, :, cols(b)], ps[:, 2, 0:DT * P].rearrange("p (d r) -> p d r", d=DT)[:, :, 0:rows(b)],
                              ACT.Copy).then_inc(hT32_ready, 1)

            def hT_hi(b):
                act.wait_ge(hT32_ready, b + 1)
                act.wait_ge(hTlo_ready, NB - L0_HT)
                s_.activation(hT[:, 0, :, cols(b)], hT32[:, :, cols(b)], ACT.Copy).then_inc(hThi_ready, 1)

            def out_t(c):
                a, w = CHUNKS[c]
                for d in range(DT):
                    act.wait_ge(t_mm, DT * c + d + 1)
                    if c:
                        act.wait_ge(tTlo_ready, c)
                    s_.activation(t32[:, d, 0:w], ps[:, T_BANKS[c][d], 0:w], ACT.Identity, bias=mb_qk[:, d:d + 1],
                                  scale=T_SCALE / (H_SCALE * W_SCALE)).then_inc(t32_ready, 1)

            def out_weight(to, bank, done, count, ready, scale=1.0):
                act.wait_ge(done, count)
                s_.activation(to, ps[:, bank, :].rearrange("p (e f) -> p e f", e=DT), ACT.Copy, scale=scale
                              ).then_inc(ready, 1)

            def out_weights(s):
                if s == 0:
                    out_weight(wn_T[:, :, :], 5, wt_mm, 1, wt_ready)
                    out_weight(cut32[1], 2, wt_mm, 2, wt_ready, W_SCALE)
                    out_weight(w_fin[:, 3], 7, wt_mm, 3, wt_ready, 1.0 / H_SCALE)
                if s == 1:
                    out_weight(cut32[0], 2, wprod_mm, 1, wprod_ready, W_SCALE)
                if s == 2:
                    out_weight(w_fin[:, 0], 5, wprod_mm, 2, wprod_ready)
                    act.wait_ge(wprod_mm, 3)
                    s_.activation(bias0[:, :], ps[:, 2, 0:D], ACT.Copy).then_inc(wprod_ready, 1)
                if s == 3:
                    act.wait_ge(wprod_mm, 4)
                    s_.activation(mb_qk[:, :], ps[:, 2, 0:DT], ACT.Copy, scale=T_SCALE).then_inc(wprod_ready, 1)
                if s == 4:
                    act.wait_ge(w_loaded["w2"], 16)
                    s_.activation(w_fin[:, 2], w_fin[:, 2], ACT.Copy, scale=1.0 / H_SCALE).then_inc(w2_ready, 1)

            def ln_centre_act(b):
                r = rows(b)
                act.wait_ge(mmean_ready, load_of(b) + 1)
                s_.activation(centred_of(b)[0:r, :], x[0:r, b, :], ACT.Relu, bias=minus_mean[0:r, b:b + 1]
                              ).then_inc(centred0_act, 1)

            for b in range(0, NB, 2):
                ln_centre_act(b)
                if b == 4:
                    ln_hi(0)
                    ln_hi(2)
                    exp0(0)
            ln_hi(4)
            ln_hi(6)
            out_pT0(0)
            exp0(1)
            ln_hi(8)
            ln_hi(10)
            for s in range(NB + L0_HT + 1):
                if s == 1:
                    out_pT0(1)
                    out_y(0)
                if 0 < s < NB - 1:
                    exp0(s + 1)
                if 1 < s < NB:
                    out_pT0(s)
                if 0 <= s - L0_TURN_Y < NB:
                    out_yT(s - L0_TURN_Y)
                if s == NB:
                    degree(0)
                if 1 <= s - 1 < NB:
                    out_y(s - 1)
                out_weights(s)
                if s < NB and 0 <= s - L0_FIN:
                    ln_hi(NB + s - L0_FIN)
                if 0 <= s - L0_HT < NB:
                    out_hT(s - L0_HT)
                    if s >= NB:
                        hT_hi(s - L0_HT)
                if s == T_STEP:
                    out_t(0)
                if s == NB + 1:
                    out_adjT(0)
                if NB <= s < NB + L0_FIN:
                    ln_hi(NB + s - L0_FIN)

            def exp1(b):
                r = rows(b)
                n = NB + b
                act.wait_ge(shift_ready, n + 1)
                if b >= 2:
                    act.wait_ge(p_turned, n - 1)
                    act.wait_ge(plo_ready, b - 1)
                s_.activation(p_hi[0:r, b % 2, :], logits[0:r, b % 2, :], ACT.Exp, bias=shift[0:r, n:n + 1]
                              ).then_inc(exp_ready, 1)
                s_.activation(p_f32[0:r, b % 2, :], logits[0:r, b % 2, :], ACT.Exp, bias=shift[0:r, n:n + 1],
                              accum_out=den[0:r, n:n + 1]).then_inc(exp32_ready, 1)

            for s in range(NB + 4):
                if 0 <= s - 3 < NB:
                    out_y(NB + s - 3)
                if 1 <= s - 2 < NB:
                    out_adjT(s - 2)
                if 0 <= s - 4 < NB:
                    ln_hi(2 * NB + s - 4)
                if 1 < s < NB:
                    degree(s)
                if 0 <= s - 3 < NB:
                    out_yT(NB + s - 3)
                if s < NB:
                    exp1(s)
                if s == 1:
                    degree(s)
                    out_t(2)
            act.wait_ge(omt_ready, 1)
            for b in range(NB):
                act.wait_ge(hT_mm, NB + b + 1)
                s_.activation(hT32[:, :, cols(b)],
                              ps[:, 6 + b % 2, 0:DT * P].rearrange("p (d r) -> p d r", d=DT)[:, :, 0:rows(b)],
                              ACT.Copy, scale=one_minus_t[:, 0:1]
                              ).then_inc(hT32_ready, 1)
            act.wait_ge(w_loaded["t"], 16)
            for c, (a, w) in enumerate(CHUNKS[1:]):
                act.wait_ge(big_mm, c + 2)
                s_.activation(yT_all[:, 1, a:a + w], ps_big[:, 1, a:a + w], ACT.Copy, scale=ts[:, 0:1]
                              ).then_inc(scaled_ready, 1)
            for b in range(NB):
                ln_hi(3 * NB + b)
            for c, (a, w) in enumerate(CHUNKS):
                act.wait_ge(big_mm, NCH + c + 1)
                s_.activation(yT_all[:, 1, a:a + w], ps_big[:, 1, a:a + w], ACT.Copy).then_inc(big_out_act, 1)

        @block.vector
        def _(dve):
            v = nc.vector

            def ln_stats(n):
                layer, b = divmod(n, NB)
                r = rows(b)
                if layer == 0:
                    dve.wait_ge(x_loaded[load_of(b)], 16)
                else:
                    dve.wait_ge(x_added, n - NB + 1)
                v.bn_stats(stats[0:r, n, :], x[0:r, b, :]).then_inc(stats_ready, 1)
                if layer:
                    ln_aggr(n)

            def ln_aggr(n):
                r = rows(n % NB)
                dve.wait_ge(stats_ready, n + 1)
                v.bn_aggr(mean_var[0:r, n, :], stats[0:r, n, :]).then_inc(mv_ready, 1)

            def ln_centre(n):
                layer, b = divmod(n, NB)
                r = rows(b)
                dve.wait_ge(mv_ready, n + 1)
                if n >= NB + RING:
                    dve.wait_ge(lo_ready, n - RING + 1)
                v.tensor_scalar(centred_of(n)[0:r, :], x[0:r, b, :], mean_var[0:r, n, 0:1], 0.0,
                                ALU.subtract, ALU.max).then_inc(centred_ready, 1)

            def ln_lo(n):
                layer, b = divmod(n, NB)
                r = rows(b)
                wait_hi(dve, n)
                wait_centred(dve, n)
                if layer >= 2:
                    dve.wait_ge(y_mm, NB * (layer - 1))
                v.scalar_tensor_tensor(out=h_parts[0:r, layer % 2, b, 1, :], in0=centred_of(n)[0:r, :],
                                       scalar=rstd[0:r, n:n + 1], in1=h_parts[0:r, layer % 2, b, 0, :],
                                       op0=ALU.mult, op1=ALU.subtract).then_inc(lo_ready, 1)

            def max0(b):
                r = rows(b)
                adj_landed(dve, b)
                v.tensor_reduce(row_max[0:r, b:b + 1], adj_rows[0:r, b % 3, :], AX.X, ALU.max).then_inc(max_ready, 1)
                dve.wait_ge(max_ready, b + 1)
                v.tensor_scalar(shift[0:r, b:b + 1], row_max[0:r, b:b + 1], -NEG, None, ALU.mult
                                ).then_inc(shift_ready, 1)

            def out_pT(n):
                b = n % NB
                to = pT[:, n % 2, :].rearrange("p (k j i) -> p k j i", k=2, i=P)
                src = ps_turned[b % 2].rearrange("p (k j) i -> p k j i", k=2)
                dve.wait_ge(p_turned, n + 1)
                dve.wait_ge(y_mm, n - 1)
                v.tensor_copy(to[:, :, 0:NB - 1, 0:rows(b)], src[:, :, 0:NB - 1, 0:rows(b)])
                v.tensor_copy(to[0:LAST, :, NB - 1, 0:rows(b)], src[0:LAST, :, NB - 1, 0:rows(b)]).then_inc(pT_ready, 1)

            def inverse(n):
                r = rows(n % NB)
                if n < NB:
                    dve.wait_ge(exp_ready, n + 1)
                else:
                    dve.wait_ge(exp32_ready, n - NB + 1)
                v.reciprocal(rden[0:r, n:n + 1], den[0:r, n:n + 1]).then_inc(rden_ready, 1)

            def hT_lo(b):
                dve.wait_ge(hThi_ready, b + 1)
                v.tensor_tensor(hT[:, 1, :, cols(b)], hT32[:, :, cols(b)], hT[:, 0, :, cols(b)],
                                ALU.subtract).then_inc(hTlo_ready, 1)

            def t_lo(c):
                a, w = CHUNKS[c]
                dve.wait_ge(t32_ready, 2 * c + 2)
                dve.wait_ge(tThi_ready, c + 1)
                v.tensor_tensor(tT[:, 1, :, a:a + w], t32[:, :, 0:w], tT[:, 0, :, a:a + w],
                                ALU.subtract).then_inc(tTlo_ready, 1)

            def add0(b):
                r = rows(b)
                dve.wait_ge(fin_mm, b + 1)
                if b == 0:
                    dve.wait_ge(wprod_ready, 3)
                if b >= 2:
                    dve.wait_ge(x_added, b - 1)
                v.tensor_tensor(head_out[0:r, b % 2, :], ps[0:r, 5, 0:D], bias0[0:r, :], ALU.add
                                ).then_inc(head_ready, 1)
                dve.wait_ge(head_ready, b + 1)
                v.scalar_tensor_tensor(out=x[0:r, b, :], in0=head_out[0:r, b % 2, :], scalar=0.0, in1=x[0:r, b, :],
                                       op0=ALU.max, op1=ALU.add).then_inc(x_added, 1)

            for at in TRIPLES:
                v.memset(ps_flat[:, at + (NB - 1) * P // 2:at + NB * P // 2], 0.0).then_inc(ps_cleared, 1)
            for b in range(NB):
                ln_stats(b)
                if b:
                    ln_aggr(b - 1)
                if b == BPC + 3:
                    max0(0)
            ln_aggr(NB - 1)
            ln_centre(1)
            ln_centre(3)
            max0(1)
            for b in range(5, NB, 2):
                ln_centre(b)
            for b in range(NB):
                ln_lo(b)
            inverse(0)
            for s in range(NB + L0_HT + 1):
                if s < NB - 2:
                    max0(s + 2)
                if 0 <= s - L0_FIN < NB:
                    add0(s - L0_FIN)
                    ln_stats(NB + s - L0_FIN)
                    ln_centre(NB + s - L0_FIN)
                if 0 < s < NB:
                    inverse(s)
                if 0 <= s - L0_FIN - 1 < NB:
                    ln_lo(NB + s - L0_FIN - 1)
                if NB <= s < NB + L0_HT:
                    hT_lo(s - L0_HT)
                if s == T_STEP + 1:
                    t_lo(0)

            def logits_max(b):
                r = rows(b)
                n = NB + b
                dve.wait_ge(scores_mm, b + 1)
                dve.wait_ge(adj_scaled_ready, b + 1)
                if b >= 2:
                    dve.wait_ge(exp32_ready, b - 1)
                v.tensor_tensor_reduce(logits[0:r, b % 2, :], ps_scores[b % 2][0:r, :], adj_scaled[0:r, b % 2, :],
                                       1.0 / S_UNIT, -3.0e38, ALU.add, ALU.max, row_max[0:r, n:n + 1]
                                       ).then_inc(max_ready, 1)
                dve.wait_ge(max_ready, n + 1)
                v.tensor_scalar(shift[0:r, n:n + 1], row_max[0:r, n:n + 1], -1.0, LN2_15, ALU.mult, ALU.add
                                ).then_inc(shift_ready, 1)

            def p_low(b):
                r = rows(b)
                n = NB + b
                dve.wait_ge(exp_ready, n + 1)
                dve.wait_ge(exp32_ready, b + 1)
                if b >= 2:
                    dve.wait_ge(p_turned, n - 1)
                v.tensor_tensor(p_lo[0:r, b % 2, :], p_f32[0:r, b % 2, :], p_hi[0:r, b % 2, :], ALU.subtract
                                ).then_inc(plo_ready, 1)

            def y_low(b):
                r = rows(b)
                n = NB + b
                dve.wait_ge(y_ready, n + 1)
                dve.wait_ge(rden_ready, n + 1)
                v.scalar_tensor_tensor(out=y16[0:r, n % 2, 1, :], in0=ps_y[0:r, :], scalar=rden[0:r, n:n + 1],
                                       in1=y16[0:r, n % 2, 0, :], op0=ALU.mult, op1=ALU.subtract
                                       ).then_inc(ylo_ready, 1)

            def add1(b):
                r = rows(b)
                dve.wait_ge(fin_mm, NB + b + 1)
                dve.wait_ge(xb_ready, b + 1)
                v.scalar_tensor_tensor(out=x[0:r, b, :], in0=ps[0:r, 7, 0:D], scalar=1.0 / (H_SCALE * W_SCALE),
                                       in1=x[0:r, b, :], op0=ALU.mult, op1=ALU.add).then_inc(x_added, 1)

            for s in range(NB + 4):
                if 0 <= s - 3 < NB:
                    y_low(s - 3)
                if 0 <= s - 4 < NB:
                    add1(s - 4)
                    ln_stats(2 * NB + s - 4)
                    ln_centre(2 * NB + s - 4)
                if s == 0:
                    logits_max(0)
                    logits_max(1)
                    a, w = CHUNKS[1]
                    for d in range(DT):
                        dve.wait_ge(t_mm, DT + d + 1)
                        dve.wait_ge(tTlo_ready, 1)
                        v.tensor_scalar(t32[:, d, 0:w], ps[:, T_BANKS[1][d], 0:w], T_SCALE / (H_SCALE * W_SCALE),
                                        mb_qk[:, d:d + 1], ALU.mult, ALU.add).then_inc(t32_ready, 1)
                if 2 <= s < NB:
                    logits_max(s)
                if 0 <= s - 4 < NB:
                    ln_lo(2 * NB + s - 4)
                if 0 <= s - 1 < NB:
                    out_pT(NB + s - 1)
                if 0 <= s - 1 < NCH - 1:
                    t_lo(s)
                if s < NB:
                    p_low(s)
                    inverse(NB + s)

            dve.wait_ge(w_loaded["t"], 16)
            dve.wait_ge(hT32_ready, 2 * NB)

            def out_sums2(c):
                a, w = CHUNKS[c]
                dve.wait_ge(big_mm, c + 1)
                for d in range(DT if c == 0 else 1):
                    v.scalar_tensor_tensor(out=yT_all[:, d, a:a + w], in0=ps_big[:, d, a:a + w], scalar=ts[:, 0:1],
                                           in1=hT32[:, d, a:a + w], op0=ALU.mult, op1=ALU.add).then_inc(big_out, 1)

            out_sums2(0)
            out_sums2(1)
            for b in range(NB + 2):
                if b < NB:
                    r = rows(b)
                    dve.wait_ge(fin_mm, 2 * NB + b + 1)
                    v.tensor_tensor(x[0:r, b, :], ps[0:r, 6 + b % 2, 0:D], x[0:r, b, :], ALU.add).then_inc(x_added, 1)
                if b == 0:
                    out_sums2(2)
                if 0 <= b - 1 < NB:
                    ln_stats(3 * NB + b - 1)
                    ln_centre(3 * NB + b - 1)
                if 0 <= b - 2:
                    ln_lo(3 * NB + b - 2)
            for c, (a, w) in enumerate(CHUNKS):
                dve.wait_ge(big_mm, NCH + c + 1)
                v.tensor_copy(yT_all[:, 0, a:a + w], ps_big[:, 0, a:a + w]).then_inc(big_out, 1)
            for b in range(NB):
                r = rows(b)
                dve.wait_ge(fin_mm, 3 * NB + b + 1)
                dve.wait_ge(xb_ready, NB + b + 1)
                v.scalar_tensor_tensor(out=x[0:r, b, :], in0=ps[0:r, 6 + b % 2, 0:D], scalar=dis[0:r, b:b + 1],
                                       in1=x[0:r, b, :], op0=ALU.mult, op1=ALU.add).then_inc(x_added, 1)

        @block.tensor
        def _(pe):
            t = nc.tensor

            def turn_weight(name, bank):
                pe.wait_ge(w_loaded[name], 16)
                for e in range(DT):
                    for d in range(DT):
                        last = t.transpose(ps[:, bank, e * D + d * P:e * D + (d + 1) * P],
                                           square[name][:, d, e * P:(e + 1) * P], ident32[:, :])
                last.then_inc(wt_mm, 1)

            def product(out_of, lhs, rhs):
                for m, o in enumerate(out_of):
                    for e in range(DT):
                        last = t.matmul(o, lhs(e, m), rhs(e), start=(e == 0), stop=(e == DT - 1))
                last.then_inc(wprod_mm, 1)

            def tile_of(w):
                return lambda e, m: w[:, e, m * P:(m + 1) * P]

            def prepare_weights(s):
                if s == 0:
                    turn_weight("w_node", 5)
                    turn_weight("wv", 2)
                    turn_weight("w3", 7)
                if s == 1:
                    pe.wait_ge(wt_ready, 2)
                    pe.wait_ge(w_loaded["wq"], 16)
                    pe.wait_ge(w_loaded["wk"], 16)
                    product([ps[:, 2, d * D:(d + 1) * D] for d in range(DT)], tile_of(square["wq"]),
                            lambda e: square["wk"][:, e, :])
                if s == 2:
                    pe.wait_ge(ksum_ready, 4)
                    product([ps[:, 5, d * D:(d + 1) * D] for d in range(DT)], tile_of(wn_T), lambda e: k_sum[:, e, :])
                    pe.wait_ge(bwide_ready, DT)
                    pe.wait_ge(wprod_ready, 1)
                    product([ps[:, 2, 0:D]], lambda e, m: bnode_wide[:, e, :], lambda e: k_sum[:, e, :])
                if s == 3:
                    pe.wait_ge(wprod_ready, 3)
                    pe.wait_ge(w_loaded["bq"], 16 * DT)
                    product([ps[:, 2, d:d + 1] for d in range(DT)], tile_of(square["wk"]),
                            lambda e: bq_col[:, e:e + 1])

            def turn(dst, src, b, at):
                r = rows(b)
                for j in range(NB):
                    last = t.transpose(dst[0:rows(j), at + j, 0:r], src[0:r, cols(j)],
                                       ident16[0:r, 0:r])
                return last

            def turn0(b):
                if b >= 2:
                    pe.wait_ge(pT_ready, b - 1)
                pe.wait_ge(exp_ready, b + 1)
                turn(ps_turned[b % 2], p_hi[:, b % 2, :], b, 0).then_inc(p_turned, 1)

            def turn_adj(b):
                if b == 0:
                    pe.wait_ge(pT_ready, NB - 1)
                elif b < NB - 1:
                    pe.wait_ge(logits_ready, NB + b + 2)
                else:
                    pe.wait_ge(pT_ready, 2 * NB - 1)
                pe.wait_ge(deg_ready, b + 1)
                turn(ps_turned[(b + 1) % 2], adj16[:, b % 2, :], b, 0).then_inc(adj_turned, 1)

            def weigh(n):
                layer, b = divmod(n, NB)
                r = rows(b)
                pe.wait_ge(pT_ready, n + 1)
                if n:
                    pe.wait_ge(y_ready, n)
                if n > NB:
                    pe.wait_ge(ylo_ready, n - NB)
                if n == NB:
                    pe.wait_ge(lo_ready, 2 * NB)
                    pe.wait_ge(t32_ready, DT * NCH)
                terms = [(0, 0), (0, 1)] + [(1, 0)] * layer
                for j in range(NB):
                    if n == 0:
                        pe.wait_ge(lo_ready, j + 1)
                    for k, (pp, hp) in enumerate(terms):
                        tile = pT[0:rows(j), n % 2, (pp * NB + j) * P:(pp * NB + j) * P + r]
                        last = t.matmul(ps_y[0:r, :], tile, h_parts[0:rows(j), layer % 2, j, hp, :],
                                        start=(j == 0 and k == 0), stop=(j == NB - 1 and k == len(terms) - 1))
                last.then_inc(y_mm, 1)

            def turn_y(n):
                r = rows(n % NB)
                pe.wait_ge(y_ready, n + 1)
                if n >= NB + 1:
                    pe.wait_ge(x_added, n)
                elif n:
                    pe.wait_ge(yT_ready, n)
                else:
                    pe.wait_ge(wt_ready, 3)
                if n < NB:
                    for d in range(DT):
                        last = t.transpose(ps_yT[:, d, 0:r], y_rows[0:r, n % 2, d * P:(d + 1) * P], ident32[0:r, 0:r])
                else:
                    pe.wait_ge(ylo_ready, n - NB + 1)
                    for part in range(2):
                        for d in range(DT):
                            last = t.transpose(ps_yT16[:, part * DT + d, 0:r],
                                               y16[0:r, n % 2, part, d * P:(d + 1) * P], ident16[0:r, 0:r])
                last.then_inc(y_turned, 1)

            def final(n, bank, left):
                layer, b = divmod(n, NB)
                r = rows(b)
                for d in range(DT):
                    last = t.matmul(ps[0:r, bank, 0:D], left(d), w_fin[:, layer, d, :],
                                    start=(d == 0), stop=(d == DT - 1))
                last.then_inc(fin_mm, 1)

            def final_att(n, bank):
                pe.wait_ge(yT_ready, n + 1)
                if n == 0:
                    pe.wait_ge(wprod_ready, 2)
                if bank == 5 and n:
                    pe.wait_ge(head_ready, n)
                    if n + L0_FIN > T_STEP:
                        pe.wait_ge(t32_ready, 1)
                if n < NB:
                    final(n, bank, lambda d: yT[:, n % 2, d, 0:rows(n % NB)])
                    return
                r = rows(n % NB)
                if n == NB:
                    pe.wait_ge(cut_lo_ready, 1)
                terms = [(d, yp, wp) for d in range(DT) for yp, wp in ((0, 0), (0, 1), (1, 0))]
                for k, (d, yp, wp) in enumerate(terms):
                    last = t.matmul(ps[0:r, bank, 0:D], yT16[:, n % 2, yp * DT + d, 0:r], wv_T[:, wp, d, :],
                                    start=(k == 0), stop=(k == len(terms) - 1))
                last.then_inc(fin_mm, 1)

            def turn_h(n, bank):
                layer, b = divmod(n, NB)
                r = rows(b)
                pe.wait_ge(lo_ready, n + 1)
                for d in range(DT):
                    for part in range(2):
                        last = t.matmul(ps[:, bank, d * P:d * P + r],
                                        h_parts[0:r, layer % 2, b, part, d * P:(d + 1) * P],
                                        ident16[0:r, 0:r], start=(part == 0), stop=(part == 1))
                last.then_inc(hT_mm, 1)

            def make_t(c):
                a, w = CHUNKS[c]
                last_block = min((c + 1) * BPC, NB)
                pe.wait_ge(hTlo_ready, last_block)
                pe.wait_ge(cut_lo_ready, 2)
                pe.wait_ge(head_ready, min(last_block + L0_HT - L0_FIN + 1, NB))
                if c:
                    pe.wait_ge(yT_ready, NB)
                for m in range(DT):
                    if c == 0 and m == 1:
                        pe.wait_ge(hT32_ready, T_STEP - L0_HT + 1)
                    if c > 1:
                        pe.wait_ge(t32_ready, DT * (c - 1) + m + 1)
                    terms = [(d, mp, hp) for d in range(DT) for mp, hp in ((0, 0), (0, 1), (1, 0))]
                    for k, (d, mp, hp) in enumerate(terms):
                        last = t.matmul(ps[:, T_BANKS[c][m], 0:w], m_qk[:, mp, d, m * P:(m + 1) * P],
                                        hT[:, hp, d, a:a + w], start=(k == 0), stop=(k == len(terms) - 1))
                    last.then_inc(t_mm, 1)

            def scores(b, chunks):
                r = rows(b)
                pe.wait_ge(pT_ready, NB if b == 0 else NB + b - 1)
                if b == 0 and NCH - 1 in chunks:
                    pe.wait_ge(hT32_ready, NB)
                if b == 1:
                    pe.wait_ge(adjT_ready, 1)
                    if NCH - 1 in chunks:
                        pe.wait_ge(head_ready, NB)
                pe.wait_ge(tTlo_ready, b // BPC + 1)
                for c in chunks:
                    a, w = CHUNKS[c]
                    if b <= 1:
                        pe.wait_ge(hTlo_ready, min((c + 1) * BPC, NB))
                    terms = [(d, tp, hp) for d in range(DT) for tp, hp in ((0, 0), (0, 1), (1, 0))]
                    for k, (d, tp, hp) in enumerate(terms):
                        last = t.matmul(ps[0:r, 3 * (b % 2) + c, 0:w], tT[:, tp, d, cols(b)], hT[:, hp, d, a:a + w],
                                        start=(k == 0), stop=(k == len(terms) - 1))
                if NCH - 1 in chunks:
                    last.then_inc(scores_mm, 1)

            def gather(layer, j):
                par, r = layer % 2, rows(j)
                if layer == 2 and j == 0:
                    pe.wait_ge(logits_ready, 2 * NB)
                    pe.wait_ge(pT_ready, 2 * NB)
                    pe.wait_ge(adjT_ready, NB)
                pe.wait_ge(lo_ready, layer * NB + j + 1)
                if j < NB - 1:
                    for d in range(DT):
                        for part in range(2):
                            left = h_parts[0:r, par, j, part, d * P:(d + 1) * P]
                            for a, w in CHUNKS:
                                t.matmul(ps_big[:, d, a:a + w], left, adjT[0:r, j, a:a + w],
                                         start=(j == 0 and part == 0), stop=False)
                    return
                for a, w in CHUNKS:
                    for d in range(DT):
                        for part in range(2):
                            left = h_parts[0:r, par, j, part, d * P:(d + 1) * P]
                            last = t.matmul(ps_big[:, d, a:a + w], left, adjT[0:r, j, a:a + w],
                                            start=False, stop=(part == 1))
                    last.then_inc(big_mm, 1)

            pe.wait_ge(ident_ready, 4)
            pe.wait_ge(ps_cleared, 2)
            for s in range(NB + L0_HT + 1):
                if 0 <= s - L0_FIN < NB:
                    final_att(s - L0_FIN, 5)
                if s in (1, 2):
                    weigh(s - 1)
                if s < NB:
                    turn0(s)
                if s == 0:
                    prepare_weights(0)
                if 0 <= s - L0_TURN_Y < NB:
                    turn_y(s - L0_TURN_Y)
                if 2 <= s - 1 < NB:
                    weigh(s - 1)
                if s:
                    prepare_weights(s)
                if s == NB + 1:
                    turn_adj(0)
                if s == NB + 2:
                    scores(0, [0])
                if s == NB + 3:
                    scores(0, [1])
                b = s - L0_HT
                if 0 <= b < NB:
                    if b == 0:
                        pe.wait_ge(wprod_ready, 4)
                    else:
                        pe.wait_ge(hT32_ready, b)
                        if s > T_STEP:
                            pe.wait_ge(t32_ready, DT)
                    turn_h(NB + b, 2)
                if s == T_STEP:
                    make_t(0)
                if s == NB + 2:
                    scores(1, [0])
                if s == NB + 4:
                    scores(1, [1])

            def turn1(b):
                n = NB + b
                if b:
                    pe.wait_ge(adjT_ready, b)
                pe.wait_ge(exp_ready, n + 1)
                turn(ps_turned[b % 2], p_hi[:, b % 2, :], b, 0)
                if b == 0:
                    make_t(2)
                pe.wait_ge(plo_ready, b + 1)
                turn(ps_turned[b % 2], p_lo[:, b % 2, :], b, NB).then_inc(p_turned, 1)

            for s in range(NB + 4):
                if 0 <= s - 4 < NB:
                    final_att(NB + s - 4, 7)
                if s == 0:
                    scores(0, [NCH - 1])
                    scores(1, [NCH - 1])
                    make_t(1)
                if 2 <= s < NB:
                    scores(s, range(NCH))
                if s == NB:
                    turn_y(NB + s - 3)
                if 0 <= s - 1 < NB:
                    turn1(s - 1)
                if 0 <= s - 3 and s < NB:
                    turn_y(NB + s - 3)
                if 0 <= s - 2 and s <= NB:
                    weigh(NB + s - 2)
                if s == NB + 1:
                    weigh(NB + s - 2)
                    turn_y(NB + s - 3)
                    gather(2, 0)
                if s == NB + 2:
                    gather(2, 1)
                    turn_y(NB + s - 3)
                    gather(2, 2)
                if 1 <= s - 1 < NB:
                    turn_adj(s - 1)
            for j in range(NB):
                if j == 1:
                    pe.wait_ge(x_added, 2 * NB)
                if j >= 2:
                    pe.wait_ge(hT32_ready, NB + j - 1)
                turn_h(2 * NB + j, 6 + j % 2)
                if j % 2 == 0 and EARLY + j // 2 < NB:
                    gather(2, EARLY + j // 2)
            for j in range(EARLY + (NB + 1) // 2, NB):
                gather(2, j)

            def final_big(layer, b):
                c = b // BPC
                if layer == 2:
                    pe.wait_ge(big_out, DT + c)
                    if c:
                        pe.wait_ge(big_out_pool, c)
                    if b == 0:
                        pe.wait_ge(w2_ready, 1)
                else:
                    pe.wait_ge(big_out, DT + NCH - 1 + c + 1)
                    pe.wait_ge(big_out_act, c + 1)
                if b >= 2:
                    pe.wait_ge(x_added, layer * NB + b - 1)
                final(layer * NB + b, 6 + b % 2, lambda d: yT_all[:, d, cols(b)])

            nxt = BPC + 1
            for b in range(nxt):
                final_big(2, b)
            pe.wait_ge(big_out, DT + NCH - 1)
            pe.wait_ge(scaled_ready, NCH - 1)
            for j in range(NB):
                gather(3, j)
                for b in range(nxt, min(nxt + 2, NB)):
                    final_big(2, b)
                nxt += 2
            pe.wait_ge(x_added, 3 * NB)
            for b in range(NB):
                final_big(3, b)


INS = ["x", "adj", "L0_gnn_W_node", "L0_gnn_b_node", "L0_gnn_K", "L1_gnn_Wq", "L1_gnn_bq", "L1_gnn_Wk",
       "L1_gnn_Wv", "L1_gnn_bv", "L2_gnn_t", "L2_gnn_weight", "L3_gnn_W", "L3_gnn_b"]


def kernel(**inputs):
    import numpy as np
    import concourse.bacc as bacc
    from concourse.bass_utils import run_bass_kernel_spmd

    nc = bacc.Bacc("TRN2", target_bir_lowering=False, num_devices=1)
    arrays, args = {}, []
    for name in INS:
        a = np.ascontiguousarray(inputs[name])
        arrays[f"in_{name}"] = a
        args.append(nc.dram_tensor(f"in_{name}", a.shape, mybir.dt.from_np(a.dtype), kind="ExternalInput").ap())
    args.append(nc.dram_tensor("out_x", inputs["x"].shape, F32, kind="ExternalOutput").ap())
    build(nc, *args)
    r = run_bass_kernel_spmd(nc, [arrays], core_ids=[0])
    return r.results[0]["out_x"]
```
